# Optimizing a Trainium2 kernel written in Bass

```python
import numpy as np
import jax
import jax.numpy as jnp

def _softmax(x, axis=-1):
    return jax.nn.softmax(x, axis=axis)

def _gelu(x):
    return jax.nn.gelu(x, approximate=True)

def _silu(x):
    return jax.nn.silu(x)

def _sigmoid(x):
    return jax.nn.sigmoid(x)

def _layernorm(x, axis=-1, eps=1e-05):
    m = jnp.mean(x, axis=axis, keepdims=True)
    v = jnp.var(x, axis=axis, keepdims=True)
    return (x - m) / jnp.sqrt(v + eps)

def _scatter_add(tgt, idx, src, axis=0):
    return tgt.at[idx].add(src)

def _segment_sum(src, seg, n):
    return jax.ops.segment_sum(src, seg, n)
kernel_name = 'mk_prb_d1_jaxref_r2_24aaca'

def setup_inputs(seed: int=0):
    np.random.seed(seed)
    _w = jnp.asarray

    def _L0_attn_setup():
        import jax, jax.numpy as jnp
        import numpy as np
        EMB = 512
        HEADS = 16
        HEAD_DIM = EMB // HEADS
        key = jax.random.key(seed)
        ks = jax.random.split(key, 5)
        B, N = (2, 1024)
        x = jax.random.normal(ks[0], (B, N, EMB), dtype=jnp.float32)
        lim_qkv = 1.0 / np.sqrt(EMB)
        qkv_w = jax.random.uniform(ks[1], (3 * EMB, EMB), minval=-lim_qkv, maxval=lim_qkv, dtype=jnp.float32)
        qkv_b = jax.random.uniform(ks[2], (3 * EMB,), minval=-lim_qkv, maxval=lim_qkv, dtype=jnp.float32)
        proj_w = jax.random.uniform(ks[3], (EMB, EMB), minval=-lim_qkv, maxval=lim_qkv, dtype=jnp.float32)
        proj_b = jax.random.uniform(ks[4], (EMB,), minval=-lim_qkv, maxval=lim_qkv, dtype=jnp.float32)
        return {'x': x, 'qkv_w': qkv_w, 'qkv_b': qkv_b, 'proj_w': proj_w, 'proj_b': proj_b}
    _L0_attn_in = _L0_attn_setup()

    def _L0_ffn_setup():
        import jax, jax.numpy as jnp
        import numpy as np
        TOP_K = 2
        key = jax.random.key(seed)
        ks = jax.random.split(key, 6)
        B, S, D, E = (8, 2048, 512, 8)
        s = 1.0 / np.sqrt(D)
        return {'x': jax.random.normal(ks[0], (B, S, D), dtype=jnp.float32), 'Wr': jax.random.normal(ks[1], (D, E), dtype=jnp.float32) * s, 'br': jnp.zeros((E,), dtype=jnp.float32), 'W1': jax.random.normal(ks[2], (E, D, D), dtype=jnp.float32) * s, 'b1': jnp.zeros((E, D), dtype=jnp.float32), 'W2': jax.random.normal(ks[3], (E, D, D), dtype=jnp.float32) * s, 'b2': jnp.zeros((E, D), dtype=jnp.float32)}
    _L0_ffn_in = _L0_ffn_setup()
    _d = {'L0_attn_x': _L0_attn_in['x'], 'L0_attn_qkv_w': _L0_attn_in['qkv_w'], 'L0_attn_qkv_b': _L0_attn_in['qkv_b'], 'L0_attn_proj_w': _L0_attn_in['proj_w'], 'L0_attn_proj_b': _L0_attn_in['proj_b'], 'L0_ffn_Wr': _L0_ffn_in['Wr'], 'L0_ffn_br': _L0_ffn_in['br'], 'L0_ffn_W1': _L0_ffn_in['W1'], 'L0_ffn_b1': _L0_ffn_in['b1'], 'L0_ffn_W2': _L0_ffn_in['W2'], 'L0_ffn_b2': _L0_ffn_in['b2']}
    _x0 = _d['L0_attn_x']
    _d['L0_attn_x'] = jax.random.normal(jax.random.fold_in(jax.random.key(seed), 1), (4, 2048, 512), dtype=_x0.dtype)
    del _x0
    return _d

def reference(L0_attn_x, L0_attn_qkv_w, L0_attn_qkv_b, L0_attn_proj_w, L0_attn_proj_b, L0_ffn_Wr, L0_ffn_br, L0_ffn_W1, L0_ffn_b1, L0_ffn_W2, L0_ffn_b2):

    def _L0_attn_ref(x, qkv_w, qkv_b, proj_w, proj_b):
        import jax, jax.numpy as jnp
        import numpy as np
        EMB = 512
        HEADS = 16
        HEAD_DIM = EMB // HEADS
        B, N, C = x.shape
        scale = HEAD_DIM ** (-0.5)
        qkv = jnp.einsum('bnc,dc->bnd', x, qkv_w) + qkv_b
        qkv = qkv.reshape(B, N, 3, HEADS, HEAD_DIM).transpose(2, 0, 3, 1, 4)
        q, k, v = (qkv[0], qkv[1], qkv[2])
        attn = jnp.einsum('bhqd,bhkd->bhqk', q, k) * scale
        attn = jax.nn.softmax(attn, axis=-1)
        out = jnp.einsum('bhqk,bhkd->bhqd', attn, v)
        out = out.transpose(0, 2, 1, 3).reshape(B, N, C)
        return jnp.einsum('bnc,dc->bnd', out, proj_w) + proj_b

    def _L0_ffn_ref(x, Wr, br, W1, b1, W2, b2):
        import jax, jax.numpy as jnp
        import numpy as np
        TOP_K = 2
        k = TOP_K
        scores0 = x[:, 0, :] @ Wr + br
        _, idx = jax.lax.top_k(scores0, k)
        W1g, b1g = (W1[idx], b1[idx])
        W2g, b2g = (W2[idx], b2[idx])
        h = jnp.einsum('bsd,bkde->bkse', x, W1g) + b1g[:, :, None, :]
        h = jax.nn.gelu(h, approximate=False)
        o = jnp.einsum('bkse,bkef->bksf', h, W2g) + b2g[:, :, None, :]
        return jnp.sum(o, axis=1) / k
    x = L0_attn_x
    xn = _layernorm(x, axis=-1)
    x = x + _L0_attn_ref(xn, L0_attn_qkv_w, L0_attn_qkv_b, L0_attn_proj_w, L0_attn_proj_b) + _L0_ffn_ref(xn, L0_ffn_Wr, L0_ffn_br, L0_ffn_W1, L0_ffn_b1, L0_ffn_W2, L0_ffn_b2)
    return x

_drawn_inputs = setup_inputs


def setup_inputs(seed=0):
    import zlib

    import numpy as np

    out = dict(_drawn_inputs(seed))
    spreads = {'L0_ffn_br': (0.0, 0.1), 'L0_ffn_b1': (0.0, 0.1), 'L0_ffn_b2': (0.0, 0.1)}
    factors = {'L0_attn_qkv_w': 3.531, 'L0_attn_qkv_b': 4.175, 'L0_attn_proj_b': 3.037}
    for name, (base, spread) in spreads.items():
        noise = np.random.default_rng([zlib.crc32(name.encode()), seed]).standard_normal(out[name].shape)
        drawn = base * np.exp(spread * noise) if base else spread * noise
        out[name] = jnp.asarray(drawn.astype(out[name].dtype))
    for name, factor in factors.items():
        out[name] = (out[name] * factor).astype(out[name].dtype)
    return out
```

```python
import concourse.bass as bass
from concourse import mybir
from contextlib import ExitStack

F32 = mybir.dt.float32
F32R = mybir.dt.float32r
U32 = mybir.dt.uint32
ALU = mybir.AluOpType
ACT = mybir.ActivationFunctionType
AX = mybir.AxisListType

P = 128
B, N, C = 4, 2048, 512
H, D = 16, 32
E = 8
EPS = 1e-5
SCALE = float(D) ** -0.5
CC = C // P
TOK = 512
NCH = N // TOK
TT = TOK // P
HQ = H // 4
NQ = B * HQ
KT = N // P


def since(base, count):
    return base + max(count, 0)


def dense_stage(nc, x, x0, wqkvT, qk_bT, v_b, wr, br, w1, b1T, w2, b2, proj_b, qh_d, ql_d, kh_d, kl_d, v_d, y_d):
    NW = 3 * C
    WP = 2 * C
    ORDER = ["qk"] * 8 + ["v"] * 4 + ["h", "h", "t"] * 4
    PER = {k: ORDER.count(k) for k in ("qk", "v", "h", "t")}
    ctx = ExitStack()
    with ctx:
        def sb(name, shape, dt):
            return ctx.enter_context(nc.sbuf_tensor(name, shape, dt))

        def sem(name):
            return ctx.enter_context(nc.semaphore(name))

        wq_hi = sb("wq_hi", [P, CC, NW], F32R)
        wq_lo = sb("wq_lo", [P, CC, NW], F32R)
        we_hi = sb("we_hi", [P, 2, 2, CC, C], F32R)
        we_lo = sb("we_lo", [P, 2, 2, CC, C], F32R)
        stage = sb("stage", [P, 2, WP], F32)
        xt = sb("xt", [P, TT, C], F32)
        xnT_hi = sb("xnT_hi", [P, 2, CC, TOK], F32R)
        xnT_lo = sb("xnT_lo", [P, 2, CC, TOK], F32R)
        h_f = sb("h_f", [P, 2, TOK], F32)
        h_hi = sb("h_hi", [P, 2, TOK], F32R)
        h_lo = sb("h_lo", [P, 2, TOK], F32R)
        qk_hi = sb("qk_hi", [P, 2, TOK], F32R)
        qk_lo = sb("qk_lo", [P, 2, TOK], F32R)
        v_out = sb("v_out", [P, 2, C], F32)
        y_out = sb("y_out", [P, 2, C], F32)
        x_res = sb("x_res", [P, 2, C], F32)
        v_bias = sb("v_bias", [P, C], F32)
        p_bias = sb("p_bias", [P, C], F32)
        y_bias = sb("y_bias", [P, C], F32)
        qk_bias = sb("qk_bias", [P, 8], F32)
        b1_sb = sb("b1_sb", [P, 2, CC], F32)
        ident = sb("ident", [P, P], F32)
        stats = sb("stats", [P, TT, 6], F32)
        mean = sb("mean", [P, TT], F32)
        mean_gap = sb("mean_gap", [P, TT], F32)
        var_sum = sb("var_sum", [P, TT], F32)
        var_eps = sb("var_eps", [P, TT], F32)
        rstd = sb("rstd", [P, TT], F32)
        minus_half = sb("minus_half", [P, TT], F32)
        x0_sb = xt[0:B, 0, :]
        x0T = sb("x0T", [P, CC, B], F32)
        wr_sb = sb("wr_sb", [P, CC, E], F32)
        br_sb = sb("br_sb", [B, E], F32)
        score = sb("score", [B, E], F32)
        top = sb("top", [B, E], F32)
        top_i = sb("top_i", [B, E], U32)
        top_row = sb("top_row", [1, B * E], U32)
        rot = [ctx.enter_context(nc.psum_tensor(f"rot{i}", [P, 512], F32)) for i in range(4)]
        acc = [ctx.enter_context(nc.psum_tensor(f"acc{i}", [P, 512], F32)) for i in range(TT)]

        const_ld, x0_ld, row_ld, zeroed, ident_ok = (sem(n) for n in ("const_ld", "x0_ld", "row_ld", "zeroed", "ident_ok"))
        x0_norm, x0_tr, x0_sbd, x0_sc, x0_step, x0_top = (
            sem(n) for n in ("x0_norm", "x0_tr", "x0_sbd", "x0_sc", "x0_step", "x0_top"))
        stage_ld = [sem(f"stage_ld{i}") for i in range(2)]
        w_hi_done, w_lo_done = sem("w_hi_done"), sem("w_lo_done")
        x_ld = [sem(f"x_ld{i}") for i in range(TT)]
        ln_step, var_summed, var_ready, rstd_done, ln_done = sem("ln_step"), sem("var_summed"), sem("var_ready"), sem("rstd_done"), sem("ln_done")
        ready = {k: sem(f"{k}_ready") for k in ("qk", "v", "h", "t")}
        t_hi, t_lo = sem("t_hi"), sem("t_lo")
        qk_hi_done, qk_lo_done = sem("qk_hi_done"), sem("qk_lo_done")
        v_done, gelu_done, h_hi_done, h_lo_done, h_used = (
            sem(n) for n in ("v_done", "gelu_done", "h_hi_done", "h_lo_done", "h_used"))
        emptied = {"qk": qk_lo_done, "v": v_done, "h": gelu_done, "t": t_lo}
        o_ready, y_added, y_done = sem("o_ready"), sem("y_added"), sem("y_done")
        qk_st = [sem(f"qk_st{i}") for i in range(2)]
        v_st = [sem(f"v_st{i}") for i in range(2)]
        y_st = [sem(f"y_st{i}") for i in range(2)]
        res_ld = [sem(f"res_ld{i}") for i in range(2)]
        b1_ld, bias_half, bias_done = sem("b1_ld"), sem("bias_half"), sem("bias_done")

        NPRE = CC * NW // WP
        NEXP = 2 * 2 * CC * C // WP
        wq_flat = [w[:, :, :].rearrange("p c n -> p (c n)") for w in (wq_hi, wq_lo)]
        we_flat = [w[:, :, :, :, :].rearrange("p e m c n -> p (e m c n)") for w in (we_hi, we_lo)]

        def used_bank(b, i, u, last):
            at = i * len(ORDER) + u - 4
            if last and at >= (NCH - 1) * len(ORDER) and ORDER[at % len(ORDER)] == "t":
                at -= 4
            kind = ORDER[at % len(ORDER)]
            count = (at // len(ORDER)) * PER[kind] + ORDER[: at % len(ORDER) + 1].count(kind)
            if kind == "t":
                return emptied[kind], since(b * NCH * PER[kind], count + TT)
            return emptied[kind], since(b * NCH * PER[kind], count)

        def used_hidden(b, i, j):
            if j == 1:
                return o_ready, b * NCH * TT + i * TT
            return h_used, since(b * NCH * 7, i * 7 + max(j - 1, 0))

        def bank_of_t(n):
            return n if n < TT else (8 + 4 + 3 * (n % TT) + 2) % 4

        def bank_of_h(j):
            return (8 + 4 + 3 * (j // 2) + j % 2) % 4

        with nc.Block() as block:

            @block.sync
            def _(sp):
                sp.dma_start(x0_sb, x0).then_inc(x0_ld, 16)
                sp.dma_start(wr_sb[:, :, :], wr.rearrange("(c p) e -> p c e", p=P)).then_inc(const_ld, 16)
                sp.dma_start(br_sb[:, :], br.partition_broadcast(B)).then_inc(const_ld, 16)
                sp.dma_start(qk_bias[:, :], qk_bT).then_inc(const_ld, 16)
                sp.dma_start(v_bias[:, :], v_b.partition_broadcast(P)).then_inc(const_ld, 16)
                sp.dma_start(p_bias[:, :], proj_b.partition_broadcast(P)).then_inc(const_ld, 16)
                for k in range(NPRE):
                    if k >= 2:
                        sp.wait_ge(w_lo_done, k - 1)
                    c, part = divmod(k * WP, NW)
                    left = min(WP, NW - part)
                    sp.dma_start(stage[:, k % 2, 0:left], wqkvT[c * P:(c + 1) * P, part:part + left]).then_inc(stage_ld[k % 2], 16)
                    if left < WP:
                        sp.dma_start(stage[:, k % 2, left:WP], wqkvT[(c + 1) * P:(c + 2) * P, 0:WP - left]).then_inc(stage_ld[k % 2], 16)
                sp.wait_ge(x0_top, 2)
                sp.dma_start(top_row[0:1, :].rearrange("p (b e) -> p b e", e=E), top_i[:, :]).then_inc(row_ld, 16)
                for t in range(TT):
                    if t == 0:
                        sp.wait_ge(x0_tr, 1)
                    sp.dma_start(xt[:, t, :], x[t * P:(t + 1) * P, :]).then_inc(x_ld[t], 16)
                for t in range(TT):
                    sp.wait_ge(ready["t"], t + 1)
                    sp.dma_start(xt[:, t, :], x[TOK + t * P:TOK + (t + 1) * P, :]).then_inc(x_ld[t], 16)
                sp.wait_ge(row_ld, 16)

                def turn(b, last):
                    pick = [sp.value_load(top_row[0:1, bass.ds(b * E + e, 1)], min_val=0, max_val=E - 1) for e in range(2)]
                    sp.wait_ge(gelu_done, b * NCH * PER["h"])
                    for e in range(2):
                        sp.dma_start(b1_sb[:, e, :], b1T[bass.ds(pick[e], 1), :, :].rearrange("a p c -> (a p) c")).then_inc(b1_ld, 16)
                    sp.wait_ge(y_added, b * NCH * TT)
                    for e in range(2):
                        sp.dma_start(x_res[:, e, :], b2[bass.ds(pick[e], 1), :].rearrange("a n -> (a n)").partition_broadcast(P)).then_inc(res_ld[e], 16)
                    for i in range(NCH):
                        tok = b * N + i * TOK
                        for m in range(8):
                            if i == 0:
                                e, mat, c2 = m // 4, m // 2 % 2, m % 2
                                sp.wait_ge(w_lo_done, b * NEXP + NPRE + m - 1)
                                src = (w1, w2)[mat][bass.ds(pick[e], 1), c2 * 2 * P:(c2 + 1) * 2 * P, :]
                                sp.dma_start(stage[:, m % 2, :].rearrange("p (c n) -> p c n", n=C),
                                             src.rearrange("a (c p) n -> (a p) c n", p=P)).then_inc(stage_ld[m % 2], 16)
                            hi_d, lo_d = ((qh_d, ql_d), (kh_d, kl_d))[m // 4]
                            dst = slice(i * TOK, (i + 1) * TOK)
                            sp.wait_ge(qk_lo_done, b * NCH * 8 + i * 8 + m + 1)
                            sp.dma_start(hi_d[bass.ds(b * HQ + m % 4, 1), :, dst].rearrange("a p n -> (a p) n"),
                                         qk_hi[:, m % 2, :].bitcast(F32)).then_inc(qk_st[m % 2], 16)
                            sp.dma_start(lo_d[bass.ds(b * HQ + m % 4, 1), :, dst].rearrange("a p n -> (a p) n"),
                                         qk_lo[:, m % 2, :].bitcast(F32)).then_inc(qk_st[m % 2], 16)
                        for t in range(TT):
                            sp.wait_ge(v_done, b * NCH * TT + i * TT + t + 1)
                            sp.dma_start(v_d[bass.ds(b * HQ, HQ), :, i * TT + t, :].rearrange("q p d -> p q d"),
                                         v_out[:, t % 2, :].rearrange("p (q d) -> p q d", d=P)).then_inc(v_st[t % 2], 16)
                        if not (last and i >= NCH - 2):
                            for t in range(TT):
                                sp.wait_ge(ready["t"], b * NCH * TT + i * TT + TT + t + 1)
                                sp.dma_start(xt[:, t, :], x[bass.ds(tok + 2 * TOK + t * P, P), :]).then_inc(x_ld[t], 16)
                        for t in range(TT):
                            if i == 0 and t < 2:
                                sp.wait_ge(bias_half, b + 1)
                            else:
                                sp.wait_ge(y_added, b * NCH * TT + i * TT + t - 1)
                            sp.dma_start(x_res[:, t % 2, :], x[bass.ds(tok + t * P, P), :]).then_inc(res_ld[t % 2], 16)
                            if t >= 2:
                                sp.wait_ge(y_done, b * NCH * TT + i * TT + t - 1)
                                sp.dma_start(y_d[bass.ds(tok + (t - 2) * P, P), :], y_out[:, t % 2, :]).then_inc(y_st[t % 2], 16)
                        for t in range(TT - 2, TT):
                            sp.wait_ge(y_done, b * NCH * TT + i * TT + t + 1)
                            sp.dma_start(y_d[bass.ds(tok + t * P, P), :], y_out[:, t % 2, :]).then_inc(y_st[t % 2], 16)

                turn(0, False)
                with sp.Fori(1, B - 1) as b:
                    turn(b, False)
                turn(B - 1, True)
                for i in range(2):
                    sp.wait_ge(qk_st[i], B * NCH * 4 * 32)
                    sp.wait_ge(v_st[i], B * NCH * TT // 2 * 16)
                    sp.wait_ge(y_st[i], B * NCH * TT // 2 * 16)

            @block.gpsimd
            def _(pool):
                pool.memset(ident[:, :], 0.0).then_inc(zeroed, 1)
                pool.wait_ge(zeroed, 1)
                pool.affine_select(out=ident[:, :], in_=ident[:, :], compare_op=ALU.not_equal, fill=1.0, base=0,
                                   pattern=[[-1, P]], channel_multiplier=1).then_inc(ident_ok, 1)

                def inverse_deviation(rows, cols, count):
                    pool.wait_ge(var_ready, count)
                    pool.tensor_tensor(rstd[0:rows, 0:cols], var_eps[0:rows, 0:cols], minus_half[0:rows, 0:cols],
                                       ALU.pow).then_inc(rstd_done, 1)

                pool.memset(minus_half[:, :], -0.5).then_inc(zeroed, 1)
                pool.wait_ge(zeroed, 2)
                inverse_deviation(B, 1, 1)
                inverse_deviation(P, TT, 2)

                def turn(b, last):
                    for i in range(NCH):
                        if not (last and i == NCH - 1):
                            inverse_deviation(P, TT, b * NCH + i + 3)
                        for j in range(8):
                            n = i * 8 + j
                            pool.wait_ge(h_hi_done, b * NCH * 8 + n + 1)
                            pool.wait_ge(*used_hidden(b, i, j))
                            pool.tensor_tensor(h_lo[:, n % 2, :], h_f[:, n % 2, :], h_hi[:, n % 2, :].bitcast(F32),
                                               ALU.subtract).then_inc(h_lo_done, 1)
                        for t in range(TT):
                            n = i * TT + t
                            if n == 0:
                                pool.wait_ge(bias_done, b + 1)
                            pool.wait_ge(y_added, b * NCH * TT + n + 1)
                            pool.tensor_tensor(y_out[:, t % 2, :], y_out[:, t % 2, :], y_bias[:, :], ALU.add).then_inc(y_done, 1)

                turn(0, False)
                with pool.Fori(1, B - 1) as b:
                    turn(b, False)
                turn(B - 1, True)

            @block.scalar
            def _(act):
                loaded = [0, 0]
                for k in range(NPRE):
                    loaded[k % 2] += 16 * (2 if (k * WP) % NW + WP > NW else 1)
                    act.wait_ge(stage_ld[k % 2], loaded[k % 2])
                    act.activation(wq_flat[0][:, k * WP:(k + 1) * WP], stage[:, k % 2, :], ACT.Copy).then_inc(w_hi_done, 1)

                def transposed_hi(b, n, s, t):
                    act.wait_ge(ready["t"], b * NCH * TT + n + 1)
                    act.activation(xnT_hi[:, s, :, t * P:(t + 1) * P],
                                   rot[bank_of_t(n)][:, :].rearrange("p (c n) -> p c n", n=P), ACT.Copy).then_inc(t_hi, 1)

                for t in range(TT):
                    transposed_hi(0, t, 0, t)

                def turn(b, last):
                    for i in range(NCH):
                        for m in range(8):
                            n = i * 8 + m
                            act.wait_ge(ready["qk"], b * NCH * 8 + n + 1)
                            if n == 0:
                                act.wait_ge(const_ld, 80)
                            act.wait_ge(qk_st[m % 2], since(b * NCH * 4 * 32, (n // 2) * 32))
                            act.activation(qk_hi[:, m % 2, :], rot[m % 4][:, :], ACT.Identity,
                                           bias=qk_bias[:, m:m + 1]).then_inc(qk_hi_done, 1)
                            if i == 0:
                                act.wait_ge(stage_ld[m % 2], loaded[m % 2] + 16 * (NEXP // 2 * b + m // 2 + 1))
                                act.wait_ge(o_ready, b * NCH * TT)
                                act.activation(we_flat[0][:, m * WP:(m + 1) * WP], stage[:, m % 2, :], ACT.Copy,
                                               scale=0.5 if m // 2 % 2 else 1.0).then_inc(w_hi_done, 1)
                        for j in range(8):
                            n = i * 8 + j
                            if n == 0:
                                act.wait_ge(b1_ld, b * 32 + 32)
                            act.wait_ge(ready["h"], b * NCH * 8 + n + 1)
                            act.wait_ge(h_lo_done, since(b * NCH * 8, n - 1))
                            act.activation(h_f[:, j % 2, :], rot[bank_of_h(j)][:, :], ACT.Gelu,
                                           bias=b1_sb[:, j // 4, j % 4:j % 4 + 1]).then_inc(gelu_done, 1)
                            if j % 2 and not (last and i == NCH - 1):
                                transposed_hi(b, i * TT + TT + j // 2, (i + 1) % 2, j // 2)

                turn(0, False)
                with act.Fori(1, B - 1) as b:
                    turn(b, False)
                turn(B - 1, True)

            @block.vector
            def _(dve):
                dve.wait_ge(x0_ld, 16)
                def combine(rows, cols, stepped, count):
                    r, c = slice(0, rows), slice(0, cols)
                    dve.wait_ge(ln_step, stepped)
                    dve.tensor_tensor(mean[r, c], stats[r, c, 1], stats[r, c, 4], ALU.add).then_inc(ln_step, 1)
                    dve.tensor_tensor(mean_gap[r, c], stats[r, c, 1], stats[r, c, 4], ALU.subtract).then_inc(ln_step, 1)
                    dve.tensor_tensor(var_sum[r, c], stats[r, c, 2], stats[r, c, 5], ALU.add).then_inc(ln_step, 1)
                    dve.wait_ge(ln_step, stepped + 3)
                    dve.scalar_tensor_tensor(out=mean_gap[r, c], in0=mean_gap[r, c], scalar=C / 4.0, in1=mean_gap[r, c],
                                             op0=ALU.mult, op1=ALU.mult).then_inc(ln_step, 1)
                    dve.tensor_scalar(mean[r, c], mean[r, c], 0.5, None, ALU.mult).then_inc(ln_step, 1)
                    dve.wait_ge(ln_step, stepped + 5)
                    dve.tensor_tensor(var_eps[r, c], var_sum[r, c], mean_gap[r, c], ALU.add).then_inc(var_summed, 1)
                    dve.wait_ge(var_summed, count)
                    dve.tensor_scalar(var_eps[r, c], var_eps[r, c], 1.0 / C, EPS, ALU.mult, ALU.add).then_inc(var_ready, 1)
                    dve.wait_ge(rstd_done, count)

                dve.bn_stats(stats[0:B, 0, :], x0_sb).then_inc(ln_step, 1)
                combine(B, 1, 1, 1)
                dve.tensor_scalar(x0_sb, x0_sb, mean[0:B, 0:1], rstd[0:B, 0:1], ALU.subtract, ALU.mult).then_inc(x0_norm, 1)
                dve.wait_ge(x0_tr, 1)
                dve.tensor_copy(x0T[:, :, :], rot[0][:, 0:CC * B].rearrange("p (c b) -> p c b", b=B)).then_inc(x0_sbd, 1)
                dve.wait_ge(x0_sc, 1)
                dve.wait_ge(const_ld, 80)
                dve.tensor_tensor(score[:, :], rot[1][0:B, 0:E], br_sb[:, :], ALU.add).then_inc(x0_step, 1)
                dve.wait_ge(x0_step, 1)
                dve.max(top[:, :], score[:, :]).then_inc(x0_top, 1)
                dve.wait_ge(x0_top, 1)
                dve.max_index(top_i[:, :], top[:, :], score[:, :]).then_inc(x0_top, 1)

                for k in range(NPRE):
                    dve.wait_ge(w_hi_done, k + 1)
                    dve.tensor_tensor(wq_flat[1][:, k * WP:(k + 1) * WP], stage[:, k % 2, :],
                                      wq_flat[0][:, k * WP:(k + 1) * WP].bitcast(F32), ALU.subtract).then_inc(w_lo_done, 1)

                def layer_norm(b, n):
                    for t in range(TT):
                        dve.wait_ge(x_ld[t], b * NCH * 16 + (n + 1) * 16)
                        if t == 0:
                            dve.wait_ge(ln_done, b * NCH * TT + n * TT)
                        dve.bn_stats(stats[:, t, :], xt[:, t, :]).then_inc(ln_step, 1)
                    combine(P, TT, b * NCH * 9 + n * 9 + 6 + TT, b * NCH + n + 2)
                    for t in range(TT):
                        dve.tensor_scalar(xt[:, t, :], xt[:, t, :], mean[:, t:t + 1], rstd[:, t:t + 1],
                                          ALU.subtract, ALU.mult).then_inc(ln_done, 1)

                def transposed_lo(b, n, s, t):
                    dve.wait_ge(t_hi, b * NCH * TT + n + 1)
                    dst = slice(t * P, (t + 1) * P)
                    dve.tensor_tensor(xnT_lo[:, s, :, dst], rot[bank_of_t(n)][:, :].rearrange("p (c n) -> p c n", n=P),
                                      xnT_hi[:, s, :, dst].bitcast(F32), ALU.subtract).then_inc(t_lo, 1)

                layer_norm(0, 0)
                for t in range(TT):
                    transposed_lo(0, t, 0, t)

                def turn(b, last):
                    for i in range(NCH):
                        for m in range(8):
                            n = i * 8 + m
                            dve.wait_ge(qk_hi_done, b * NCH * 8 + n + 1)
                            dve.wait_ge(qk_st[m % 2], since(b * NCH * 4 * 32, (n // 2) * 32))
                            dve.scalar_tensor_tensor(out=qk_lo[:, m % 2, :], in0=rot[m % 4][:, :], scalar=qk_bias[:, m:m + 1],
                                                     in1=qk_hi[:, m % 2, :].bitcast(F32), op0=ALU.add,
                                                     op1=ALU.subtract).then_inc(qk_lo_done, 1)
                            if i == 0:
                                dve.wait_ge(w_hi_done, NEXP * b + NPRE + m + 1)
                                dve.scalar_tensor_tensor(out=we_flat[1][:, m * WP:(m + 1) * WP], in0=stage[:, m % 2, :],
                                                         scalar=0.5 if m // 2 % 2 else 1.0,
                                                         in1=we_flat[0][:, m * WP:(m + 1) * WP].bitcast(F32),
                                                         op0=ALU.mult, op1=ALU.subtract).then_inc(w_lo_done, 1)
                        for t in range(TT):
                            n = i * TT + t
                            dve.wait_ge(ready["v"], b * NCH * TT + n + 1)
                            dve.wait_ge(v_st[t % 2], since(b * NCH * TT // 2 * 16, (n // 2) * 16))
                            dve.tensor_tensor(v_out[:, t % 2, :], rot[t % 4][:, :], v_bias[:, :], ALU.add).then_inc(v_done, 1)
                        if i == 0:
                            for e in range(2):
                                dve.wait_ge(res_ld[e], b * (NCH * TT // 2 + 1) * 16 + 16)
                            dve.wait_ge(y_done, b * NCH * TT)
                            dve.tensor_tensor(y_bias[:, :], x_res[:, 0, :], x_res[:, 1, :], ALU.add).then_inc(bias_half, 1)
                            dve.wait_ge(bias_half, b + 1)
                            dve.scalar_tensor_tensor(out=y_bias[:, :], in0=y_bias[:, :], scalar=0.5, in1=p_bias[:, :],
                                                     op0=ALU.mult, op1=ALU.add).then_inc(bias_done, 1)
                        if not (last and i == NCH - 1):
                            layer_norm(b, i + 1)
                        for j in range(8):
                            n = i * 8 + j
                            dve.wait_ge(gelu_done, b * NCH * 8 + n + 1)
                            dve.wait_ge(*used_hidden(b, i, j))
                            dve.tensor_copy(h_hi[:, j % 2, :], h_f[:, j % 2, :]).then_inc(h_hi_done, 1)
                            if j % 2 and not (last and i == NCH - 1):
                                transposed_lo(b, i * TT + TT + j // 2, (i + 1) % 2, j // 2)
                        for t in range(TT):
                            n = i * TT + t
                            dve.wait_ge(o_ready, b * NCH * TT + n + 1)
                            dve.wait_ge(res_ld[t % 2], b * (NCH * TT // 2 + 1) * 16 + (n // 2 + 2) * 16)
                            dve.wait_ge(y_st[t % 2], since(b * NCH * TT // 2 * 16, (n // 2) * 16))
                            dve.tensor_tensor(y_out[:, t % 2, :], acc[t][:, :], x_res[:, t % 2, :], ALU.add).then_inc(y_added, 1)

                turn(0, False)
                with dve.Fori(1, B - 1) as b:
                    turn(b, False)
                turn(B - 1, True)

            @block.tensor
            def _(pe):
                pe.wait_ge(ident_ok, 1)
                pe.wait_ge(x0_norm, 1)
                for c in range(CC):
                    last_op = pe.transpose(rot[0][:, c * B:(c + 1) * B], x0_sb[:, c * P:(c + 1) * P], ident[0:B, 0:B])
                last_op.then_inc(x0_tr, 1)
                pe.wait_ge(x0_sbd, 1)
                pe.wait_ge(const_ld, 80)
                for c in range(CC):
                    last_op = pe.matmul(rot[1][0:B, 0:E], x0T[:, c, :], wr_sb[:, c, :], start=(c == 0), stop=(c == CC - 1))
                last_op.then_inc(x0_sc, 1)
                pe.wait_ge(x0_step, 1)

                def transpose_tile(b, n, t):
                    pe.wait_ge(ln_done, b * NCH * TT + n + 1)
                    for c in range(CC):
                        op = pe.transpose(rot[bank_of_t(n)][:, c * P:(c + 1) * P], xt[:, t, c * P:(c + 1) * P], ident[:, :])
                    op.then_inc(ready["t"], 1)

                def split_product(out, pairs, start, stop):
                    for k, ((lh, ll), (rh, rl)) in enumerate(pairs):
                        pe.matmul(out, lh, rh, start=start and k == 0, stop=False)
                        pe.matmul(out, lh, rl, start=False, stop=False)
                        op = pe.matmul(out, ll, rh, start=False, stop=stop and k == len(pairs) - 1)
                    return op

                for t in range(TT):
                    transpose_tile(0, t, t)

                def turn(b, last):
                    for i in range(NCH):
                        s = i % 2
                        pe.wait_ge(t_hi, b * NCH * TT + (i + 1) * TT)
                        pe.wait_ge(t_lo, b * NCH * TT + (i + 1) * TT)
                        if i == 0:
                            pe.wait_ge(w_lo_done, b * NEXP + NPRE)
                        u = 0
                        for m in range(8):
                            if m > 0:
                                pe.wait_ge(*used_bank(b, i, u, last))
                            cols = slice(m * P, (m + 1) * P)
                            split_product(rot[u % 4][:, :], [((wq_hi[:, c, cols], wq_lo[:, c, cols]), (xnT_hi[:, s, c, :], xnT_lo[:, s, c, :]))
                                                             for c in range(CC)], True, True).then_inc(ready["qk"], 1)
                            u += 1
                        for t in range(TT):
                            pe.wait_ge(*used_bank(b, i, u, last))
                            rows = slice(t * P, (t + 1) * P)
                            split_product(rot[u % 4][:, :], [((xnT_hi[:, s, c, rows], xnT_lo[:, s, c, rows]), (wq_hi[:, c, 2 * C:], wq_lo[:, c, 2 * C:]))
                                                             for c in range(CC)], True, True).then_inc(ready["v"], 1)
                            u += 1
                        for j in range(9):
                            if j < 8:
                                if i == 0:
                                    pe.wait_ge(w_lo_done, b * NEXP + NPRE + (j // 4 + 1) * 4)
                                pe.wait_ge(*used_bank(b, i, u, last))
                                e, cols = j // 4, slice(j % 4 * P, (j % 4 + 1) * P)
                                split_product(rot[u % 4][:, :], [((we_hi[:, e, 0, c, cols], we_lo[:, e, 0, c, cols]), (xnT_hi[:, s, c, :], xnT_lo[:, s, c, :]))
                                                                 for c in range(CC)], True, True).then_inc(ready["h"], 1)
                                u += 1
                            if j % 2 and j < 8:
                                if not (last and i == NCH - 1):
                                    pe.wait_ge(*used_bank(b, i, u, last))
                                    transpose_tile(b, i * TT + TT + j // 2, j // 2)
                                u += 1
                            if j > 0:
                                k = j - 1
                                pe.wait_ge(h_hi_done, b * NCH * 8 + i * 8 + k + 1)
                                pe.wait_ge(h_lo_done, b * NCH * 8 + i * 8 + k + 1)
                                for t in range(TT):
                                    if k == 0:
                                        pe.wait_ge(y_added, since(b * NCH * TT, i * TT + t + 1 - TT))
                                    rows = slice(t * P, (t + 1) * P)
                                    op = split_product(acc[t][:, :], [((h_hi[:, k % 2, rows], h_lo[:, k % 2, rows]),
                                                                       (we_hi[:, k // 4, 1, k % 4, :], we_lo[:, k // 4, 1, k % 4, :]))],
                                                       k == 0, k == 7)
                                    if k == 7:
                                        op.then_inc(o_ready, 1)
                                if k < 7:
                                    op.then_inc(h_used, 1)
                        
                turn(0, False)
                with pe.Fori(1, B - 1) as b:
                    turn(b, False)
                turn(B - 1, True)


def attention_stage(nc, qh_d, ql_d, kh_d, kl_d, v_d, o_d):
    R = 3 * D
    QC = N // TOK
    UN = 4 * TT * (N // 512)
    PR = KT // 2
    ctx = ExitStack()
    with ctx:
        def sb(name, shape, dt):
            return ctx.enter_context(nc.sbuf_tensor(name, shape, dt))

        def sem(name):
            return ctx.enter_context(nc.semaphore(name))

        k_x = [sb(f"k_x{i}", [R + 1, 4, N], F32R) for i in range(2)]
        q_x = [sb(f"q_x{i}", [R + 1, 4, TOK], F32R) for i in range(QC)]
        v_sb = [sb(f"v_sb{i}", [P, KT, P], F32) for i in range(2)]
        p_sb = sb("p_sb", [P, 4, 4, TOK], F32)
        p_pair = sb("p_pair", [P, 2, 4, TOK], F32)
        ones = sb("ones", [P, D], F32)
        ident = sb("ident_b", [P, P], F32)
        unit_max = sb("unit_max", [P, 4 * TT, N // 512], F32)
        row_max = sb("row_max", [P, 4 * TT], F32)
        shift = sb("shift", [4 * TT, P], F32R)
        o_raw = sb("o_raw", [P, TOK], F32)
        sum_raw = sb("sum_raw", [P, TOK], F32)
        o_inv = sb("o_inv", [P, TOK], F32)
        o_out = sb("o_out", [P, TOK], F32)
        st_ps = ctx.enter_context(nc.psum_tensor("st_ps", [P, 2, 2, TOK], F32))
        mx_ps = [ctx.enter_context(nc.psum_tensor(f"mx_ps{i}", [P, 512], F32)) for i in range(2)]
        o_ps = ctx.enter_context(nc.psum_tensor("o_ps", [P, TOK], F32))
        sum_ps = ctx.enter_context(nc.psum_tensor("sum_ps", [P, TOK], F32))

        k_ld = [sem(f"k_ld{i}") for i in range(2)]
        q_ld = [sem(f"q_ld{i}") for i in range(QC)]
        v_ld = [sem(f"v_ld{i}") for i in range(2)]
        shift_ld, o_st = sem("shift_ld"), sem("o_st")
        zeroed, ident_ok, ones_ok = sem("zeroed_b"), sem("ident_ok_b"), sem("ones_ok")
        st_ready, unit_ready, rows_ready = sem("st_ready"), sem("unit_ready"), sem("rows_ready")
        pv_done, sum_done = sem("pv_done"), sem("sum_done")
        exp_done, o_copied, sum_copied, shift_done = sem("exp_done"), sem("o_copied"), sem("sum_copied"), sem("shift_done")
        unit_done, max_done, inv_done, o_done = sem("unit_done"), sem("max_done"), sem("inv_done"), sem("o_done")
        pair_done = sem("pair_done")

        G = 2 * QC
        TURNS = NQ // 2

        def units_of(kt):
            return range(min(10 * (kt // 2) + 6 * (kt % 2), UN), min(10 * (kt // 2) + 6 + 4 * (kt % 2), UN))

        with nc.Block() as block:

            @block.sync
            def _(sp):
                def load_keys(it, u):
                    for part, src in enumerate((kh_d, kh_d, kl_d)):
                        sp.dma_start(k_x[u][part * D:(part + 1) * D, :, :].bitcast(F32),
                                     src[it, :, :].rearrange("(h d) n -> d h n", d=D)).then_inc(k_ld[u], 16)

                def load_values(it, u):
                    sp.dma_start(v_sb[u][:, :, :], v_d[it, :, :, :]).then_inc(v_ld[u], 16)

                def load_queries(it, qc):
                    for part, src in enumerate((qh_d, ql_d, qh_d)):
                        sp.dma_start(q_x[qc][part * D:(part + 1) * D, :, :].bitcast(F32),
                                     src[it, :, qc * TOK:(qc + 1) * TOK].rearrange("(h d) n -> d h n", d=D)).then_inc(q_ld[qc], 16)

                def load_shift(count, qc):
                    sp.wait_ge(shift_done, count)
                    sp.dma_start(q_x[qc][R:R + 1, :, :].bitcast(F32),
                                 shift[:, :].bitcast(F32)).then_inc(shift_ld, 16)

                def store_group(turn0, it, qc, count):
                    dst = o_d[it, :, qc * TOK:(qc + 1) * TOK]
                    sp.lower_val(dst.offset * 4)
                    sp.wait_ge(o_done, count)
                    sp.dma_start(dst, o_out[:, :]).then_inc(o_st, 16)

                load_keys(0, 0)
                for qc in range(QC):
                    load_queries(0, qc)
                load_values(0, 0)
                load_shift(1, 0)

                def turn(L, first, last):
                    for g in range(G):
                        u, qc = g // QC, g % QC
                        it, more = L * 2 + u, not (last and u == 1)
                        if qc == 0 and more:
                            sp.wait_ge(pv_done, L * G * KT + g * KT)
                            load_keys(it + 1 if isinstance(it, int) else it + 1, 1 - u)
                            load_values(it + 1, 1 - u)
                        if qc > 0 and more:
                            sp.wait_ge(st_ready, L * G * 2 * KT + g * 2 * KT)
                            load_queries(it + 1, qc - 1)
                        if qc == 0 and not (first and u == 0):
                            sp.wait_ge(st_ready, L * G * 2 * KT + g * 2 * KT)
                            load_queries(it, QC - 1)
                        if not (last and g == G - 1):
                            load_shift(L * G + g + 2, (qc + 1) % QC)
                        if not (first and g == 0):
                            store_group(L, it - 1 if qc == 0 else it, (qc - 1) % QC, L * G + g)

                turn(0, True, False)
                with sp.Fori(1, TURNS - 1) as L:
                    turn(L, False, False)
                turn(TURNS - 1, False, True)
                store_group(0, NQ - 1, QC - 1, NQ * QC)
                sp.wait_ge(o_st, NQ * QC * 16)

            @block.gpsimd
            def _(pool):
                pool.memset(ident[:, :], 0.0).then_inc(zeroed, 1)
                pool.wait_ge(zeroed, 1)
                pool.affine_select(out=ident[:, :], in_=ident[:, :], compare_op=ALU.not_equal, fill=1.0, base=0,
                                   pattern=[[-1, P]], channel_multiplier=1).then_inc(ident_ok, 1)

                def turn(L):
                    for g in range(G):
                        for i in range(PR):
                            pool.wait_ge(exp_done, L * G * 2 * KT + g * 2 * KT + 4 * i + 4)
                            pool.wait_ge(sum_done, since(L * G * PR, g * PR + i - 1))
                            pool.tensor_tensor(p_pair[:, i % 2, :, :], p_sb[:, 2 * i % 4, :, :], p_sb[:, (2 * i + 1) % 4, :, :],
                                               ALU.add).then_inc(pair_done, 1)

                turn(0)
                with pool.Fori(1, TURNS) as L:
                    turn(L)

            @block.scalar
            def _(act):
                def turn_shift(count):
                    act.wait_ge(rows_ready, count)
                    if not (isinstance(count, int) and count == 1):
                        act.wait_ge(shift_ld, (count - 1) * 16)
                    act.activation(shift[:, :], mx_ps[0][0:4 * TT, 0:P], ACT.Copy, scale=-1.0).then_inc(shift_done, 1)

                def copy_o(count):
                    act.wait_ge(pv_done, count * KT)
                    act.wait_ge(o_done, count - 1)
                    act.activation(o_raw[:, :], o_ps[:, :], ACT.Copy).then_inc(o_copied, 1)

                def copy_sum(count):
                    act.wait_ge(sum_done, count * PR)
                    act.wait_ge(inv_done, count - 1)
                    act.activation(sum_raw[:, :], sum_ps[:, :], ACT.Copy).then_inc(sum_copied, 1)

                turn_shift(1)

                def turn(L, first, last):
                    for g in range(G):
                        for kt in range(KT):
                            n = g * KT + kt
                            for p in range(2):
                                act.wait_ge(st_ready, L * G * 2 * KT + 2 * n + p + 1)
                                act.wait_ge(pv_done, since(L * G * KT, n - 3))
                                act.wait_ge(pair_done, since(L * G * PR, (n - 4) // 2 + 1))
                                act.activation(p_sb[:, kt % 4, 2 * p:2 * p + 2, :], st_ps[:, p, :, :], ACT.Exp,
                                               scale=SCALE).then_inc(exp_done, 1)
                                if kt == 14 and p == 0 and not (last and g == G - 1):
                                    turn_shift(L * G + g + 2)
                            if kt == 0 and not (first and g == 0):
                                copy_o(L * G + g)
                            if kt == 2 and not (first and g == 0):
                                copy_sum(L * G + g)

                turn(0, True, False)
                with act.Fori(1, TURNS - 1) as L:
                    turn(L, False, False)
                turn(TURNS - 1, False, True)
                copy_o(NQ * QC)
                copy_sum(NQ * QC)

            @block.vector
            def _(dve):
                def unit(base, n):
                    dve.wait_ge(unit_ready, base + n + 1)
                    dve.reduce_max(unit_max[:, n // 4, n % 4:n % 4 + 1], mx_ps[n % 2][:, :], AX.X).then_inc(unit_done, 1)

                def rows(base, count):
                    dve.wait_ge(unit_done, base + UN)
                    dve.wait_ge(rows_ready, count - 1)
                    dve.reduce_max(row_max[:, :], unit_max[:, :, :], AX.X).then_inc(max_done, 1)

                def normalise(count):
                    dve.wait_ge(sum_copied, count)
                    dve.wait_ge(o_done, count - 1)
                    dve.reciprocal(o_inv[:, :], sum_raw[:, :]).then_inc(inv_done, 1)
                    dve.wait_ge(inv_done, count)
                    dve.wait_ge(o_copied, count)
                    dve.wait_ge(o_st, (count - 1) * 16)
                    dve.tensor_tensor(o_out[:, :], o_raw[:, :], o_inv[:, :], ALU.mult).then_inc(o_done, 1)

                for i in range(2):
                    dve.memset(k_x[i][R:R + 1, :, :].bitcast(F32), 1.0).then_inc(ones_ok, 1)
                dve.memset(ones[:, :], 1.0).then_inc(ones_ok, 1)
                for n in range(UN):
                    unit(0, n)
                rows(0, 1)

                def turn(L, first, last):
                    for g in range(G):
                        for kt in range(KT):
                            if not (last and g == G - 1):
                                base = (L * G + g + 1) * UN
                                for n in units_of(kt):
                                    if n == 0:
                                        dve.wait_ge(max_done, L * G + g + 1)
                                    unit(base, n)
                                if UN - 1 in units_of(kt):
                                    rows(base, L * G + g + 2)
                            if kt == 13 and not (first and g == 0):
                                normalise(L * G + g)

                turn(0, True, False)
                with dve.Fori(1, TURNS - 1) as L:
                    turn(L, False, False)
                turn(TURNS - 1, False, True)
                normalise(NQ * QC)

            @block.tensor
            def _(pe):
                def unit(base, n, u, qc):
                    h, t, kc = n // (4 * TT), n // 4 % TT, n % 4
                    if n >= 2:
                        pe.wait_ge(unit_done, base + n - 1)
                    pe.matmul(mx_ps[n % 2][:, :], q_x[qc][0:R, h, t * P:(t + 1) * P], k_x[u][0:R, h, kc * 512:(kc + 1) * 512],
                              start=True, stop=True).then_inc(unit_ready, 1)

                def turn_rows(count):
                    pe.wait_ge(max_done, count)
                    pe.transpose(mx_ps[0][0:4 * TT, 0:P], row_max[:, :], ident[:, :]).then_inc(rows_ready, 1)

                def values(L, n, u, kt):
                    pe.wait_ge(exp_done, L * G * 2 * KT + 2 * n + 2)
                    for h in range(4):
                        rows = slice(h * D, (h + 1) * D)
                        op = pe.matmul(o_ps[rows, :], v_sb[u][:, kt, rows], p_sb[:, kt % 4, h, :], start=(kt == 0), stop=(kt == KT - 1))
                    op.then_inc(pv_done, 1)

                def sums(L, g, i):
                    pe.wait_ge(pair_done, L * G * PR + g * PR + i + 1)
                    for h in range(4):
                        op = pe.matmul(sum_ps[h * D:(h + 1) * D, :], ones[:, :], p_pair[:, i % 2, h, :], start=(i == 0), stop=(i == PR - 1))
                    op.then_inc(sum_done, 1)

                pe.wait_ge(ident_ok, 1)
                pe.wait_ge(ones_ok, 3)
                pe.wait_ge(k_ld[0], 48)
                pe.wait_ge(q_ld[0], 48)
                for n in range(UN):
                    unit(0, n, 0, 0)
                turn_rows(1)

                def turn(L, first, last):
                    for g in range(G):
                        u, qc = g // QC, g % QC
                        nu, nq = (g + 1) % G // QC, (g + 1) % QC
                        more = not (last and g == G - 1)

                        def next_units(ns):
                            for n in ns:
                                if n == 0:
                                    pe.wait_ge(q_ld[nq], (L * 2 + u + 1 + (1 if qc == QC - 1 else 0)) * 48)
                                    pe.wait_ge(k_ld[nu], (L + 1 + (1 if g == G - 1 else 0)) * 48)
                                    pe.wait_ge(shift_done, L * G + g + 1)
                                unit((L * G + g + 1) * UN, n, nu, nq)

                        for kt in range(KT):
                            ns = units_of(kt) if more else []
                            for p in range(2):
                                next_units(ns[p:p + 1])
                                if kt == 0 and p == 0:
                                    pe.wait_ge(shift_ld, (L * G + g + 1) * 16)
                                pe.wait_ge(exp_done, since(L * G * 2 * KT, 2 * (g * KT + kt) + p - 1))
                                for h in (2 * p, 2 * p + 1):
                                    op = pe.matmul(st_ps[:, p, h % 2, :], k_x[u][:, h, kt * P:(kt + 1) * P], q_x[qc][:, h, :],
                                                   start=True, stop=True)
                                op.then_inc(st_ready, 1)
                                if kt == 14 and p == 0 and more:
                                    turn_rows(L * G + g + 2)
                            next_units(ns[2:3])
                            if kt > 0:
                                if kt == 1:
                                    pe.wait_ge(v_ld[u], (L + 1) * 16)
                                    if not (first and g == 0):
                                        pe.wait_ge(o_copied, L * G + g)
                                values(L, g * KT + kt - 1, u, kt - 1)
                            elif not (first and g == 0):
                                values(L, g * KT - 1, (g - 1) % G // QC, KT - 1)
                            next_units(ns[3:5])
                            if kt % 2 == 0:
                                if kt >= 4:
                                    if kt == 4 and not (first and g == 0):
                                        pe.wait_ge(sum_copied, L * G + g)
                                    sums(L, g, kt // 2 - 2)
                                elif not (first and g == 0):
                                    sums(L, g - 1, PR - 2 + kt // 2)
                            next_units(ns[5:6])

                turn(0, True, False)
                with pe.Fori(1, TURNS - 1) as L:
                    turn(L, False, False)
                turn(TURNS - 1, False, True)
                values(TURNS - 1, G * KT - 1, 1, KT - 1)
                sums(TURNS - 1, G - 1, PR - 2)
                sums(TURNS - 1, G - 1, PR - 1)


def output_stage(nc, proj_wT, o_d, y_d, out):
    NC2 = B * NCH
    ctx = ExitStack()
    with ctx:
        def sb(name, shape, dt):
            return ctx.enter_context(nc.sbuf_tensor(name, shape, dt))

        def sem(name):
            return ctx.enter_context(nc.semaphore(name))

        w_f = sb("w_f", [P, CC, C], F32)
        w_hi = sb("w_hi", [P, CC, C], F32R)
        w_lo = sb("w_lo", [P, CC, C], F32R)
        o_in = sb("o_in", [P, 4, CC, TOK], F32)
        o_hi = sb("o_hi", [P, 2, CC, TOK], F32R)
        o_lo = sb("o_lo", [P, 2, CC, TOK], F32R)
        y_in = sb("y_in", [P, 4, TT, C], F32)
        ps = [ctx.enter_context(nc.psum_tensor(f"ps{i}", [P, 512], F32)) for i in range(8)]
        w_ld, w_hi_done, w_lo_done = sem("w_ld"), sem("w_hi_done_c"), sem("w_lo_done_c")
        o_ld = [sem(f"o_ld{i}") for i in range(4)]
        y_ld = [sem(f"y_ld{i}") for i in range(4)]
        out_st = [sem(f"out_st{i}") for i in range(4)]
        hi_done, lo_done, prod_done, sum_done = sem("hi_done"), sem("lo_done"), sem("prod_done"), sem("out_added")

        with nc.Block() as block:

            @block.sync
            def _(sp):
                sp.dma_start(w_f[:, :, :], proj_wT.rearrange("(c p) n -> p c n", p=P)).then_inc(w_ld, 16)

                def load(b, i, s):
                    sp.dma_start(o_in[:, s, :, :], o_d[bass.ds(b * HQ, HQ), :, i * TOK:(i + 1) * TOK].rearrange("q p n -> p q n")).then_inc(o_ld[s], 16)
                    sp.dma_start(y_in[:, s, :, :], y_d[bass.ds(b * N + i * TOK, TOK), :].rearrange("(t p) n -> p t n", p=P)).then_inc(y_ld[s], 16)

                for i in range(3):
                    load(0, i, i)

                def turn(b, first, last):
                    for i in range(NCH):
                        n = i + 3
                        if not (last and n >= NCH):
                            if not (first and n < 4):
                                sp.wait_ge(out_st[n % 4], b * 16 + n // 4 * 16)
                            load(b + n // 4, n % 4, n % 4)
                        sp.wait_ge(sum_done, b * NCH * TT + (i + 1) * TT)
                        sp.dma_start(out[bass.ds(b * N + i * TOK, TOK), :].rearrange("(t p) n -> p t n", p=P), y_in[:, i, :, :]).then_inc(out_st[i], 16)

                turn(0, True, False)
                with sp.Fori(1, B - 1) as b:
                    turn(b, False, False)
                turn(B - 1, False, True)
                for s in range(4):
                    sp.wait_ge(out_st[s], B * 16)

            @block.scalar
            def _(act):
                act.wait_ge(w_ld, 16)
                act.activation(w_hi[:, :, :], w_f[:, :, :], ACT.Copy).then_inc(w_hi_done, 1)

                def turn(b):
                    for i in range(NCH):
                        act.wait_ge(o_ld[i], b * 16 + 16)
                        act.wait_ge(prod_done, since(b * NCH * TT, (i - 1) * TT))
                        for c in range(CC):
                            act.activation(o_hi[:, i % 2, c, :], o_in[:, i, c, :], ACT.Copy).then_inc(hi_done, 1)

                turn(0)
                with act.Fori(1, B) as b:
                    turn(b)

            @block.vector
            def _(dve):
                dve.wait_ge(w_hi_done, 1)
                dve.tensor_tensor(w_lo[:, :, :], w_f[:, :, :], w_hi[:, :, :].bitcast(F32), ALU.subtract).then_inc(w_lo_done, 1)

                def split(b, i):
                    dve.wait_ge(prod_done, since(b * NCH * TT, (i - 1) * TT))
                    for c in range(CC):
                        dve.wait_ge(hi_done, b * NCH * CC + i * CC + c + 1)
                        dve.tensor_tensor(o_lo[:, i % 2, c, :], o_in[:, i % 4, c, :], o_hi[:, i % 2, c, :].bitcast(F32),
                                          ALU.subtract).then_inc(lo_done, 1)

                split(0, 0)

                def turn(b, last):
                    for i in range(NCH):
                        if not (last and i == NCH - 1):
                            split(b, i + 1)
                        dve.wait_ge(y_ld[i], b * 16 + 16)
                        for t in range(TT):
                            n = i * TT + t
                            dve.wait_ge(prod_done, b * NCH * TT + n + 1)
                            dve.tensor_tensor(y_in[:, i, t, :], ps[n % 8][:, :], y_in[:, i, t, :], ALU.add).then_inc(sum_done, 1)

                turn(0, False)
                with dve.Fori(1, B - 1) as b:
                    turn(b, False)
                turn(B - 1, True)

            @block.tensor
            def _(pe):
                pe.wait_ge(w_lo_done, 1)

                def turn(b):
                    for i in range(NCH):
                        pe.wait_ge(lo_done, b * NCH * CC + (i + 1) * CC)
                        for t in range(TT):
                            n = i * TT + t
                            pe.wait_ge(sum_done, since(b * NCH * TT, n - 7))
                            rows = slice(t * P, (t + 1) * P)
                            for c in range(CC):
                                pe.matmul(ps[n % 8][:, :], o_hi[:, i % 2, c, rows], w_hi[:, c, :], start=(c == 0), stop=False)
                                pe.matmul(ps[n % 8][:, :], o_hi[:, i % 2, c, rows], w_lo[:, c, :], start=False, stop=False)
                                op = pe.matmul(ps[n % 8][:, :], o_lo[:, i % 2, c, rows], w_hi[:, c, :], start=False, stop=(c == CC - 1))
                            op.then_inc(prod_done, 1)

                turn(0)
                with pe.Fori(1, B) as b:
                    turn(b)


def block_kernel(nc, x, qkv_wT, qk_bT, v_b, proj_wT, proj_b, wr, br, w1, b1T, w2, b2, out):
    def scratch(name, shape):
        return nc.dram_tensor(name, shape, F32, kind="Internal").ap()

    qh_d, ql_d, kh_d, kl_d, o_d = (scratch(n, (NQ, P, N)) for n in ("q_hi_d", "q_lo_d", "k_hi_d", "k_lo_d", "o_d"))
    v_d = scratch("v_d", (NQ, P, KT, P))
    y_d = scratch("y_d", (B * N, C))
    x0 = x[:, 0, :]
    xf = x.rearrange("b n c -> (b n) c")
    of = out.rearrange("b n c -> (b n) c")
    dense_stage(nc, xf, x0, qkv_wT, qk_bT, v_b, wr, br, w1, b1T, w2, b2, proj_b, qh_d, ql_d, kh_d, kl_d, v_d, y_d)
    attention_stage(nc, qh_d, ql_d, kh_d, kl_d, v_d, o_d)
    output_stage(nc, proj_wT, o_d, y_d, of)


def kernel(**inputs):
    import numpy as np
    import concourse.bacc as bacc
    from concourse.bass_utils import run_bass_kernel_spmd

    a = {k: np.asarray(v) for k, v in inputs.items()}
    arrays = {
        "x": a["L0_attn_x"],
        "qkv_wT": a["L0_attn_qkv_w"].T,
        "qk_bT": a["L0_attn_qkv_b"][0:2 * C].reshape(2 * CC, P).T,
        "v_b": a["L0_attn_qkv_b"][2 * C:],
        "proj_wT": a["L0_attn_proj_w"].T,
        "proj_b": a["L0_attn_proj_b"],
        "wr": a["L0_ffn_Wr"],
        "br": a["L0_ffn_br"],
        "w1": a["L0_ffn_W1"],
        "b1T": a["L0_ffn_b1"].reshape(E, CC, P).transpose(0, 2, 1),
        "w2": a["L0_ffn_W2"],
        "b2": a["L0_ffn_b2"],
    }
    arrays = {k: np.ascontiguousarray(v) for k, v in arrays.items()}
    nc = bacc.Bacc("TRN2", target_bir_lowering=False, num_devices=1)
    args = [nc.dram_tensor(k, v.shape, mybir.dt.from_np(v.dtype), kind="ExternalInput").ap() for k, v in arrays.items()]
    args.append(nc.dram_tensor("out", (B, N, C), F32, kind="ExternalOutput").ap())
    block_kernel(nc, *args)
    r = run_bass_kernel_spmd(nc, [arrays], core_ids=[0])
    return r.results[0]["out"]
```

```python
import concourse.bass as bass
from concourse import mybir
from contextlib import ExitStack

F32 = mybir.dt.float32
F32R = mybir.dt.float32r
U32 = mybir.dt.uint32
ALU = mybir.AluOpType
ACT = mybir.ActivationFunctionType
AX = mybir.AxisListType

P = 128
B, N, C = 4, 2048, 512
H, D = 16, 32
E = 8
EPS = 1e-5
SCALE = float(D) ** -0.5
CC = C // P
TOK = 512
NCH = N // TOK
TT = TOK // P
HQ = H // 4
NQ = B * HQ
KT = N // P


def since(base, count):
    return max(base + count, 0) if isinstance(base, int) else base + count


def dense_stage(nc, x, x0, wqkvT, qk_bT, v_b, wr, br, w1, b1T, w2, b2, proj_b, qh_d, ql_d, kh_d, kl_d, v_d, y_d):
    NW = 3 * C
    WP = 2 * C
    ORDER = ["qk"] * 8 + ["v"] * 4 + ["h", "h", "t"] * 4
    PER = {k: ORDER.count(k) for k in ("qk", "v", "h", "t")}
    ctx = ExitStack()
    with ctx:
        def sb(name, shape, dt):
            return ctx.enter_context(nc.sbuf_tensor(name, shape, dt))

        def sem(name):
            return ctx.enter_context(nc.semaphore(name))

        wq_hi = sb("wq_hi", [P, CC, NW], F32R)
        wq_lo = sb("wq_lo", [P, CC, NW], F32R)
        we_hi = sb("we_hi", [P, 2, 2, CC, C], F32R)
        we_lo = sb("we_lo", [P, 2, 2, CC, C], F32R)
        stage = sb("stage", [P, 2, WP], F32)
        xt = sb("xt", [P, TT, C], F32)
        xnT_hi = sb("xnT_hi", [P, 2, CC, TOK], F32R)
        xnT_lo = sb("xnT_lo", [P, 2, CC, TOK], F32R)
        h_f = sb("h_f", [P, 2, TOK], F32)
        h_hi = sb("h_hi", [P, 2, TOK], F32R)
        h_lo = sb("h_lo", [P, 2, TOK], F32R)
        qk_hi = sb("qk_hi", [P, 2, TOK], F32R)
        qk_lo = sb("qk_lo", [P, 2, TOK], F32R)
        v_out = sb("v_out", [P, 2, C], F32)
        y_out = sb("y_out", [P, 2, C], F32)
        x_res = sb("x_res", [P, 2, C], F32)
        v_bias = sb("v_bias", [P, C], F32)
        p_bias = sb("p_bias", [P, C], F32)
        y_bias = sb("y_bias", [P, C], F32)
        qk_bias = sb("qk_bias", [P, 8], F32)
        b1_sb = sb("b1_sb", [P, 2, CC], F32)
        ident = sb("ident", [P, P], F32)
        stats = sb("stats", [P, TT, 6], F32)
        mean = sb("mean", [P, TT], F32)
        mean_gap = sb("mean_gap", [P, TT], F32)
        var_sum = sb("var_sum", [P, TT], F32)
        var_eps = sb("var_eps", [P, TT], F32)
        rstd = sb("rstd", [P, TT], F32)
        minus_half = sb("minus_half", [P, TT], F32)
        x0_sb = xt[0:B, 0, :]
        x0T = sb("x0T", [P, CC, B], F32)
        wr_sb = sb("wr_sb", [P, CC, E], F32)
        br_sb = sb("br_sb", [B, E], F32)
        score = sb("score", [B, E], F32)
        top = sb("top", [B, E], F32)
        top_i = sb("top_i", [B, E], U32)
        top_row = sb("top_row", [1, B * E], U32)
        rot = [ctx.enter_context(nc.psum_tensor(f"rot{i}", [P, 512], F32)) for i in range(4)]
        acc = [ctx.enter_context(nc.psum_tensor(f"acc{i}", [P, 512], F32)) for i in range(TT)]

        const_ld, x0_ld, row_ld, zeroed, ident_ok = (sem(n) for n in ("const_ld", "x0_ld", "row_ld", "zeroed", "ident_ok"))
        x0_norm, x0_tr, x0_sbd, x0_sc, x0_step, x0_top = (
            sem(n) for n in ("x0_norm", "x0_tr", "x0_sbd", "x0_sc", "x0_step", "x0_top"))
        stage_ld = [sem(f"stage_ld{i}") for i in range(2)]
        w_hi_done, w_lo_done = sem("w_hi_done"), sem("w_lo_done")
        x_ld = [sem(f"x_ld{i}") for i in range(TT)]
        ln_step, var_summed, var_ready, rstd_done, ln_done = sem("ln_step"), sem("var_summed"), sem("var_ready"), sem("rstd_done"), sem("ln_done")
        ready = {k: sem(f"{k}_ready") for k in ("qk", "v", "h", "t")}
        t_hi, t_lo = sem("t_hi"), sem("t_lo")
        qk_hi_done, qk_lo_done = sem("qk_hi_done"), sem("qk_lo_done")
        v_done, gelu_done, h_hi_done, h_lo_done, h_used = (
            sem(n) for n in ("v_done", "gelu_done", "h_hi_done", "h_lo_done", "h_used"))
        emptied = {"qk": qk_lo_done, "v": v_done, "h": gelu_done, "t": t_lo}
        o_ready, y_added, y_done = sem("o_ready"), sem("y_added"), sem("y_done")
        qk_st = [sem(f"qk_st{i}") for i in range(2)]
        v_st = [sem(f"v_st{i}") for i in range(2)]
        y_st = [sem(f"y_st{i}") for i in range(2)]
        res_ld = [sem(f"res_ld{i}") for i in range(2)]
        b1_ld, bias_half, bias_done = sem("b1_ld"), sem("bias_half"), sem("bias_done")

        NPRE = CC * NW // WP
        NEXP = 2 * 2 * CC * C // WP
        wq_flat = [w[:, :, :].rearrange("p c n -> p (c n)") for w in (wq_hi, wq_lo)]
        we_flat = [w[:, :, :, :, :].rearrange("p e m c n -> p (e m c n)") for w in (we_hi, we_lo)]

        def used_bank(b, i, u, last):
            at = i * len(ORDER) + u - 4
            if last and at >= (NCH - 1) * len(ORDER) and ORDER[at % len(ORDER)] == "t":
                at -= 4
            kind = ORDER[at % len(ORDER)]
            count = (at // len(ORDER)) * PER[kind] + ORDER[: at % len(ORDER) + 1].count(kind)
            if kind == "t":
                return emptied[kind], since(b * NCH * PER[kind], count + TT)
            return emptied[kind], since(b * NCH * PER[kind], count)

        def used_hidden(b, i, j):
            if j == 1:
                return o_ready, b * NCH * TT + i * TT
            return h_used, since(b * NCH * 7, i * 7 + max(j - 1, 0))

        def bank_of_t(n):
            return n if n < TT else (8 + 4 + 3 * (n % TT) + 2) % 4

        def bank_of_h(j):
            return (8 + 4 + 3 * (j // 2) + j % 2) % 4

        with nc.Block() as block:

            @block.sync
            def _(sp):
                sp.dma_start(x0_sb, x0).then_inc(x0_ld, 16)
                sp.dma_start(wr_sb[:, :, :], wr.rearrange("(c p) e -> p c e", p=P)).then_inc(const_ld, 16)
                sp.dma_start(br_sb[:, :], br.partition_broadcast(B)).then_inc(const_ld, 16)
                sp.dma_start(qk_bias[:, :], qk_bT).then_inc(const_ld, 16)
                sp.dma_start(v_bias[:, :], v_b.partition_broadcast(P)).then_inc(const_ld, 16)
                sp.dma_start(p_bias[:, :], proj_b.partition_broadcast(P)).then_inc(const_ld, 16)
                for k in range(NPRE):
                    if k >= 2:
                        sp.wait_ge(w_lo_done, k - 1)
                    c, part = divmod(k * WP, NW)
                    left = min(WP, NW - part)
                    sp.dma_start(stage[:, k % 2, 0:left], wqkvT[c * P:(c + 1) * P, part:part + left]).then_inc(stage_ld[k % 2], 16)
                    if left < WP:
                        sp.dma_start(stage[:, k % 2, left:WP], wqkvT[(c + 1) * P:(c + 2) * P, 0:WP - left]).then_inc(stage_ld[k % 2], 16)
                sp.wait_ge(x0_top, 2)
                sp.dma_start(top_row[0:1, :].rearrange("p (b e) -> p b e", e=E), top_i[:, :]).then_inc(row_ld, 16)
                for t in range(TT):
                    if t == 0:
                        sp.wait_ge(x0_tr, 1)
                    sp.dma_start(xt[:, t, :], x[t * P:(t + 1) * P, :]).then_inc(x_ld[t], 16)
                for t in range(TT):
                    sp.wait_ge(ready["t"], t + 1)
                    sp.dma_start(xt[:, t, :], x[TOK + t * P:TOK + (t + 1) * P, :]).then_inc(x_ld[t], 16)
                sp.wait_ge(row_ld, 16)

                def turn(b, last):
                    pick = [sp.value_load(top_row[0:1, bass.ds(b * E + e, 1)], min_val=0, max_val=E - 1) for e in range(2)]
                    sp.wait_ge(gelu_done, b * NCH * PER["h"])
                    for e in range(2):
                        sp.dma_start(b1_sb[:, e, :], b1T[bass.ds(pick[e], 1), :, :].rearrange("a p c -> (a p) c")).then_inc(b1_ld, 16)
                    sp.wait_ge(y_added, b * NCH * TT)
                    for e in range(2):
                        sp.dma_start(x_res[:, e, :], b2[bass.ds(pick[e], 1), :].rearrange("a n -> (a n)").partition_broadcast(P)).then_inc(res_ld[e], 16)
                    for i in range(NCH):
                        tok = b * N + i * TOK
                        for m in range(8):
                            if i == 0:
                                e, mat, c2 = m // 4, m // 2 % 2, m % 2
                                sp.wait_ge(w_lo_done, b * NEXP + NPRE + m - 1)
                                src = (w1, w2)[mat][bass.ds(pick[e], 1), c2 * 2 * P:(c2 + 1) * 2 * P, :]
                                sp.dma_start(stage[:, m % 2, :].rearrange("p (c n) -> p c n", n=C),
                                             src.rearrange("a (c p) n -> (a p) c n", p=P)).then_inc(stage_ld[m % 2], 16)
                            hi_d, lo_d = ((qh_d, ql_d), (kh_d, kl_d))[m // 4]
                            dst = slice(i * TOK, (i + 1) * TOK)
                            sp.wait_ge(qk_lo_done, b * NCH * 8 + i * 8 + m + 1)
                            sp.dma_start(hi_d[bass.ds(b * HQ + m % 4, 1), :, dst].rearrange("a p n -> (a p) n"),
                                         qk_hi[:, m % 2, :].bitcast(F32)).then_inc(qk_st[m % 2], 16)
                            sp.dma_start(lo_d[bass.ds(b * HQ + m % 4, 1), :, dst].rearrange("a p n -> (a p) n"),
                                         qk_lo[:, m % 2, :].bitcast(F32)).then_inc(qk_st[m % 2], 16)
                        for t in range(TT):
                            sp.wait_ge(v_done, b * NCH * TT + i * TT + t + 1)
                            sp.dma_start(v_d[bass.ds(b * HQ, HQ), :, i * TT + t, :].rearrange("q p d -> p q d"),
                                         v_out[:, t % 2, :].rearrange("p (q d) -> p q d", d=P)).then_inc(v_st[t % 2], 16)
                        if not (last and i >= NCH - 2):
                            for t in range(TT):
                                sp.wait_ge(ready["t"], b * NCH * TT + i * TT + TT + t + 1)
                                sp.dma_start(xt[:, t, :], x[bass.ds(tok + 2 * TOK + t * P, P), :]).then_inc(x_ld[t], 16)
                        for t in range(TT):
                            if i == 0 and t < 2:
                                sp.wait_ge(bias_half, b + 1)
                            else:
                                sp.wait_ge(y_added, b * NCH * TT + i * TT + t - 1)
                            sp.dma_start(x_res[:, t % 2, :], x[bass.ds(tok + t * P, P), :]).then_inc(res_ld[t % 2], 16)
                            if t >= 2:
                                sp.wait_ge(y_done, b * NCH * TT + i * TT + t - 1)
                                sp.dma_start(y_d[bass.ds(tok + (t - 2) * P, P), :], y_out[:, t % 2, :]).then_inc(y_st[t % 2], 16)
                        for t in range(TT - 2, TT):
                            sp.wait_ge(y_done, b * NCH * TT + i * TT + t + 1)
                            sp.dma_start(y_d[bass.ds(tok + t * P, P), :], y_out[:, t % 2, :]).then_inc(y_st[t % 2], 16)

                turn(0, False)
                with sp.Fori(1, B - 1) as b:
                    turn(b, False)
                turn(B - 1, True)
                for i in range(2):
                    sp.wait_ge(qk_st[i], B * NCH * 4 * 32)
                    sp.wait_ge(v_st[i], B * NCH * TT // 2 * 16)
                    sp.wait_ge(y_st[i], B * NCH * TT // 2 * 16)

            @block.gpsimd
            def _(pool):
                pool.memset(ident[:, :], 0.0).then_inc(zeroed, 1)
                pool.wait_ge(zeroed, 1)
                pool.affine_select(out=ident[:, :], in_=ident[:, :], compare_op=ALU.not_equal, fill=1.0, base=0,
                                   pattern=[[-1, P]], channel_multiplier=1).then_inc(ident_ok, 1)

                def inverse_deviation(rows, cols, count):
                    pool.wait_ge(var_ready, count)
                    pool.tensor_tensor(rstd[0:rows, 0:cols], var_eps[0:rows, 0:cols], minus_half[0:rows, 0:cols],
                                       ALU.pow).then_inc(rstd_done, 1)

                pool.memset(minus_half[:, :], -0.5).then_inc(zeroed, 1)
                pool.wait_ge(zeroed, 2)
                inverse_deviation(B, 1, 1)
                inverse_deviation(P, TT, 2)

                def turn(b, last):
                    for i in range(NCH):
                        if not (last and i == NCH - 1):
                            inverse_deviation(P, TT, b * NCH + i + 3)
                        for j in range(8):
                            n = i * 8 + j
                            pool.wait_ge(h_hi_done, b * NCH * 8 + n + 1)
                            pool.wait_ge(*used_hidden(b, i, j))
                            pool.tensor_tensor(h_lo[:, n % 2, :], h_f[:, n % 2, :], h_hi[:, n % 2, :].bitcast(F32),
                                               ALU.subtract).then_inc(h_lo_done, 1)
                        for t in range(TT):
                            n = i * TT + t
                            if n == 0:
                                pool.wait_ge(bias_done, b + 1)
                            pool.wait_ge(y_added, b * NCH * TT + n + 1)
                            pool.tensor_tensor(y_out[:, t % 2, :], y_out[:, t % 2, :], y_bias[:, :], ALU.add).then_inc(y_done, 1)

                turn(0, False)
                with pool.Fori(1, B - 1) as b:
                    turn(b, False)
                turn(B - 1, True)

            @block.scalar
            def _(act):
                loaded = [0, 0]
                for k in range(NPRE):
                    loaded[k % 2] += 16 * (2 if (k * WP) % NW + WP > NW else 1)
                    act.wait_ge(stage_ld[k % 2], loaded[k % 2])
                    act.activation(wq_flat[0][:, k * WP:(k + 1) * WP], stage[:, k % 2, :], ACT.Copy).then_inc(w_hi_done, 1)

                def transposed_hi(b, n, s, t):
                    act.wait_ge(ready["t"], b * NCH * TT + n + 1)
                    act.activation(xnT_hi[:, s, :, t * P:(t + 1) * P],
                                   rot[bank_of_t(n)][:, :].rearrange("p (c n) -> p c n", n=P), ACT.Copy).then_inc(t_hi, 1)

                for t in range(TT):
                    transposed_hi(0, t, 0, t)

                def turn(b, last):
                    for i in range(NCH):
                        for m in range(8):
                            n = i * 8 + m
                            act.wait_ge(ready["qk"], b * NCH * 8 + n + 1)
                            if n == 0:
                                act.wait_ge(const_ld, 80)
                            act.wait_ge(qk_st[m % 2], since(b * NCH * 4 * 32, (n // 2) * 32))
                            act.activation(qk_hi[:, m % 2, :], rot[m % 4][:, :], ACT.Identity,
                                           bias=qk_bias[:, m:m + 1]).then_inc(qk_hi_done, 1)
                            if i == 0:
                                act.wait_ge(stage_ld[m % 2], loaded[m % 2] + 16 * (NEXP // 2 * b + m // 2 + 1))
                                act.wait_ge(o_ready, b * NCH * TT)
                                act.activation(we_flat[0][:, m * WP:(m + 1) * WP], stage[:, m % 2, :], ACT.Copy,
                                               scale=0.5 if m // 2 % 2 else 1.0).then_inc(w_hi_done, 1)
                        for j in range(8):
                            n = i * 8 + j
                            if n == 0:
                                act.wait_ge(b1_ld, b * 32 + 32)
                            act.wait_ge(ready["h"], b * NCH * 8 + n + 1)
                            act.wait_ge(h_lo_done, since(b * NCH * 8, n - 1))
                            act.activation(h_f[:, j % 2, :], rot[bank_of_h(j)][:, :], ACT.Gelu,
                                           bias=b1_sb[:, j // 4, j % 4:j % 4 + 1]).then_inc(gelu_done, 1)
                            if j % 2 and not (last and i == NCH - 1):
                                transposed_hi(b, i * TT + TT + j // 2, (i + 1) % 2, j // 2)

                turn(0, False)
                with act.Fori(1, B - 1) as b:
                    turn(b, False)
                turn(B - 1, True)

            @block.vector
            def _(dve):
                dve.wait_ge(x0_ld, 16)
                def combine(rows, cols, stepped, count):
                    r, c = slice(0, rows), slice(0, cols)
                    dve.wait_ge(ln_step, stepped)
                    dve.tensor_tensor(mean[r, c], stats[r, c, 1], stats[r, c, 4], ALU.add).then_inc(ln_step, 1)
                    dve.tensor_tensor(mean_gap[r, c], stats[r, c, 1], stats[r, c, 4], ALU.subtract).then_inc(ln_step, 1)
                    dve.tensor_tensor(var_sum[r, c], stats[r, c, 2], stats[r, c, 5], ALU.add).then_inc(ln_step, 1)
                    dve.wait_ge(ln_step, stepped + 3)
                    dve.scalar_tensor_tensor(out=mean_gap[r, c], in0=mean_gap[r, c], scalar=C / 4.0, in1=mean_gap[r, c],
                                             op0=ALU.mult, op1=ALU.mult).then_inc(ln_step, 1)
                    dve.tensor_scalar(mean[r, c], mean[r, c], 0.5, None, ALU.mult).then_inc(ln_step, 1)
                    dve.wait_ge(ln_step, stepped + 5)
                    dve.tensor_tensor(var_eps[r, c], var_sum[r, c], mean_gap[r, c], ALU.add).then_inc(var_summed, 1)
                    dve.wait_ge(var_summed, count)
                    dve.tensor_scalar(var_eps[r, c], var_eps[r, c], 1.0 / C, EPS, ALU.mult, ALU.add).then_inc(var_ready, 1)
                    dve.wait_ge(rstd_done, count)

                dve.bn_stats(stats[0:B, 0, :], x0_sb).then_inc(ln_step, 1)
                combine(B, 1, 1, 1)
                dve.tensor_scalar(x0_sb, x0_sb, mean[0:B, 0:1], rstd[0:B, 0:1], ALU.subtract, ALU.mult).then_inc(x0_norm, 1)
                dve.wait_ge(x0_tr, 1)
                dve.tensor_copy(x0T[:, :, :], rot[0][:, 0:CC * B].rearrange("p (c b) -> p c b", b=B)).then_inc(x0_sbd, 1)
                dve.wait_ge(x0_sc, 1)
                dve.wait_ge(const_ld, 80)
                dve.tensor_tensor(score[:, :], rot[1][0:B, 0:E], br_sb[:, :], ALU.add).then_inc(x0_step, 1)
                dve.wait_ge(x0_step, 1)
                dve.max(top[:, :], score[:, :]).then_inc(x0_top, 1)
                dve.wait_ge(x0_top, 1)
                dve.max_index(top_i[:, :], top[:, :], score[:, :]).then_inc(x0_top, 1)

                for k in range(NPRE):
                    dve.wait_ge(w_hi_done, k + 1)
                    dve.tensor_tensor(wq_flat[1][:, k * WP:(k + 1) * WP], stage[:, k % 2, :],
                                      wq_flat[0][:, k * WP:(k + 1) * WP].bitcast(F32), ALU.subtract).then_inc(w_lo_done, 1)

                def layer_norm(b, n):
                    for t in range(TT):
                        dve.wait_ge(x_ld[t], b * NCH * 16 + (n + 1) * 16)
                        if t == 0:
                            dve.wait_ge(ln_done, b * NCH * TT + n * TT)
                        dve.bn_stats(stats[:, t, :], xt[:, t, :]).then_inc(ln_step, 1)
                    combine(P, TT, b * NCH * 9 + n * 9 + 6 + TT, b * NCH + n + 2)
                    for t in range(TT):
                        dve.tensor_scalar(xt[:, t, :], xt[:, t, :], mean[:, t:t + 1], rstd[:, t:t + 1],
                                          ALU.subtract, ALU.mult).then_inc(ln_done, 1)

                def transposed_lo(b, n, s, t):
                    dve.wait_ge(t_hi, b * NCH * TT + n + 1)
                    dst = slice(t * P, (t + 1) * P)
                    dve.tensor_tensor(xnT_lo[:, s, :, dst], rot[bank_of_t(n)][:, :].rearrange("p (c n) -> p c n", n=P),
                                      xnT_hi[:, s, :, dst].bitcast(F32), ALU.subtract).then_inc(t_lo, 1)

                layer_norm(0, 0)
                for t in range(TT):
                    transposed_lo(0, t, 0, t)

                def turn(b, last):
                    for i in range(NCH):
                        for m in range(8):
                            n = i * 8 + m
                            dve.wait_ge(qk_hi_done, b * NCH * 8 + n + 1)
                            dve.wait_ge(qk_st[m % 2], since(b * NCH * 4 * 32, (n // 2) * 32))
                            dve.scalar_tensor_tensor(out=qk_lo[:, m % 2, :], in0=rot[m % 4][:, :], scalar=qk_bias[:, m:m + 1],
                                                     in1=qk_hi[:, m % 2, :].bitcast(F32), op0=ALU.add,
                                                     op1=ALU.subtract).then_inc(qk_lo_done, 1)
                            if i == 0:
                                dve.wait_ge(w_hi_done, NEXP * b + NPRE + m + 1)
                                dve.scalar_tensor_tensor(out=we_flat[1][:, m * WP:(m + 1) * WP], in0=stage[:, m % 2, :],
                                                         scalar=0.5 if m // 2 % 2 else 1.0,
                                                         in1=we_flat[0][:, m * WP:(m + 1) * WP].bitcast(F32),
                                                         op0=ALU.mult, op1=ALU.subtract).then_inc(w_lo_done, 1)
                        for t in range(TT):
                            n = i * TT + t
                            dve.wait_ge(ready["v"], b * NCH * TT + n + 1)
                            dve.wait_ge(v_st[t % 2], since(b * NCH * TT // 2 * 16, (n // 2) * 16))
                            dve.tensor_tensor(v_out[:, t % 2, :], rot[t % 4][:, :], v_bias[:, :], ALU.add).then_inc(v_done, 1)
                        if i == 0:
                            for e in range(2):
                                dve.wait_ge(res_ld[e], b * (NCH * TT // 2 + 1) * 16 + 16)
                            dve.wait_ge(y_done, b * NCH * TT)
                            dve.tensor_tensor(y_bias[:, :], x_res[:, 0, :], x_res[:, 1, :], ALU.add).then_inc(bias_half, 1)
                            dve.wait_ge(bias_half, b + 1)
                            dve.scalar_tensor_tensor(out=y_bias[:, :], in0=y_bias[:, :], scalar=0.5, in1=p_bias[:, :],
                                                     op0=ALU.mult, op1=ALU.add).then_inc(bias_done, 1)
                        if not (last and i == NCH - 1):
                            layer_norm(b, i + 1)
                        for j in range(8):
                            n = i * 8 + j
                            dve.wait_ge(gelu_done, b * NCH * 8 + n + 1)
                            dve.wait_ge(*used_hidden(b, i, j))
                            dve.tensor_copy(h_hi[:, j % 2, :], h_f[:, j % 2, :]).then_inc(h_hi_done, 1)
                            if j % 2 and not (last and i == NCH - 1):
                                transposed_lo(b, i * TT + TT + j // 2, (i + 1) % 2, j // 2)
                        for t in range(TT):
                            n = i * TT + t
                            dve.wait_ge(o_ready, b * NCH * TT + n + 1)
                            dve.wait_ge(res_ld[t % 2], b * (NCH * TT // 2 + 1) * 16 + (n // 2 + 2) * 16)
                            dve.wait_ge(y_st[t % 2], since(b * NCH * TT // 2 * 16, (n // 2) * 16))
                            dve.tensor_tensor(y_out[:, t % 2, :], acc[t][:, :], x_res[:, t % 2, :], ALU.add).then_inc(y_added, 1)

                turn(0, False)
                with dve.Fori(1, B - 1) as b:
                    turn(b, False)
                turn(B - 1, True)

            @block.tensor
            def _(pe):
                pe.wait_ge(ident_ok, 1)
                pe.wait_ge(x0_norm, 1)
                for c in range(CC):
                    last_op = pe.transpose(rot[0][:, c * B:(c + 1) * B], x0_sb[:, c * P:(c + 1) * P], ident[0:B, 0:B])
                last_op.then_inc(x0_tr, 1)
                pe.wait_ge(x0_sbd, 1)
                pe.wait_ge(const_ld, 80)
                for c in range(CC):
                    last_op = pe.matmul(rot[1][0:B, 0:E], x0T[:, c, :], wr_sb[:, c, :], start=(c == 0), stop=(c == CC - 1))
                last_op.then_inc(x0_sc, 1)
                pe.wait_ge(x0_step, 1)

                def transpose_tile(b, n, t):
                    pe.wait_ge(ln_done, b * NCH * TT + n + 1)
                    for c in range(CC):
                        op = pe.transpose(rot[bank_of_t(n)][:, c * P:(c + 1) * P], xt[:, t, c * P:(c + 1) * P], ident[:, :])
                    op.then_inc(ready["t"], 1)

                def split_product(out, pairs, start, stop):
                    for k, ((lh, ll), (rh, rl)) in enumerate(pairs):
                        pe.matmul(out, lh, rh, start=start and k == 0, stop=False)
                        pe.matmul(out, lh, rl, start=False, stop=False)
                        op = pe.matmul(out, ll, rh, start=False, stop=stop and k == len(pairs) - 1)
                    return op

                for t in range(TT):
                    transpose_tile(0, t, t)

                def turn(b, last):
                    for i in range(NCH):
                        s = i % 2
                        pe.wait_ge(t_hi, b * NCH * TT + (i + 1) * TT)
                        pe.wait_ge(t_lo, b * NCH * TT + (i + 1) * TT)
                        if i == 0:
                            pe.wait_ge(w_lo_done, b * NEXP + NPRE)
                        u = 0
                        for m in range(8):
                            if m > 0:
                                pe.wait_ge(*used_bank(b, i, u, last))
                            cols = slice(m * P, (m + 1) * P)
                            split_product(rot[u % 4][:, :], [((wq_hi[:, c, cols], wq_lo[:, c, cols]), (xnT_hi[:, s, c, :], xnT_lo[:, s, c, :]))
                                                             for c in range(CC)], True, True).then_inc(ready["qk"], 1)
                            u += 1
                        for t in range(TT):
                            pe.wait_ge(*used_bank(b, i, u, last))
                            rows = slice(t * P, (t + 1) * P)
                            split_product(rot[u % 4][:, :], [((xnT_hi[:, s, c, rows], xnT_lo[:, s, c, rows]), (wq_hi[:, c, 2 * C:], wq_lo[:, c, 2 * C:]))
                                                             for c in range(CC)], True, True).then_inc(ready["v"], 1)
                            u += 1
                        for j in range(9):
                            if j < 8:
                                if i == 0:
                                    pe.wait_ge(w_lo_done, b * NEXP + NPRE + (j // 4 + 1) * 4)
                                pe.wait_ge(*used_bank(b, i, u, last))
                                e, cols = j // 4, slice(j % 4 * P, (j % 4 + 1) * P)
                                split_product(rot[u % 4][:, :], [((we_hi[:, e, 0, c, cols], we_lo[:, e, 0, c, cols]), (xnT_hi[:, s, c, :], xnT_lo[:, s, c, :]))
                                                                 for c in range(CC)], True, True).then_inc(ready["h"], 1)
                                u += 1
                            if j % 2 and j < 8:
                                if not (last and i == NCH - 1):
                                    pe.wait_ge(*used_bank(b, i, u, last))
                                    transpose_tile(b, i * TT + TT + j // 2, j // 2)
                                u += 1
                            if j > 0:
                                k = j - 1
                                pe.wait_ge(h_hi_done, b * NCH * 8 + i * 8 + k + 1)
                                pe.wait_ge(h_lo_done, b * NCH * 8 + i * 8 + k + 1)
                                for t in range(TT):
                                    if k == 0:
                                        pe.wait_ge(y_added, since(b * NCH * TT, i * TT + t + 1 - TT))
                                    rows = slice(t * P, (t + 1) * P)
                                    op = split_product(acc[t][:, :], [((h_hi[:, k % 2, rows], h_lo[:, k % 2, rows]),
                                                                       (we_hi[:, k // 4, 1, k % 4, :], we_lo[:, k // 4, 1, k % 4, :]))],
                                                       k == 0, k == 7)
                                    if k == 7:
                                        op.then_inc(o_ready, 1)
                                if k < 7:
                                    op.then_inc(h_used, 1)
                        
                turn(0, False)
                with pe.Fori(1, B - 1) as b:
                    turn(b, False)
                turn(B - 1, True)


def attention_stage(nc, qh_d, ql_d, kh_d, kl_d, v_d, o_d):
    R = 3 * D
    QC = N // TOK
    UN = 4 * TT * (N // 512)
    PR = KT // 2
    SLOTS = 8
    AHEAD = 13
    ADDS = [0, 1, "four", 2, 3, 4, 5, "four", 6, 7]
    PARTS = [(3, 1, 7), (4, 0, 9), (5, 1, 11), (8, 1, 15), (9, 0, 17), (10, 1, 19)]
    NA, NS = len(ADDS), len(PARTS)
    ctx = ExitStack()
    with ctx:
        def sb(name, shape, dt):
            return ctx.enter_context(nc.sbuf_tensor(name, shape, dt))

        def sem(name):
            return ctx.enter_context(nc.semaphore(name))

        k_x = [sb(f"k_x{i}", [R + 1, 4, N], F32R) for i in range(2)]
        q_x = [sb(f"q_x{i}", [R + 1, 4, TOK], F32R) for i in range(QC)]
        v_sb = [sb(f"v_sb{i}", [P, KT, P], F32) for i in range(2)]
        p_sb = sb("p_sb", [P, SLOTS, 4, TOK], F32)
        p_pair = sb("p_pair", [P, 2, 4, TOK], F32)
        ones = sb("ones", [P, D], F32)
        ident = sb("ident_b", [P, P], F32)
        unit_max = sb("unit_max", [P, 4 * TT, N // 512], F32)
        row_max = sb("row_max", [P, 4 * TT], F32)
        shift = sb("shift", [4 * TT, P], F32R)
        o_raw = sb("o_raw", [P, TOK], F32)
        sum_raw = sb("sum_raw", [P, TOK], F32)
        o_inv = sb("o_inv", [P, TOK], F32)
        o_out = sb("o_out", [P, TOK], F32)
        st_ps = [ctx.enter_context(nc.psum_tensor(f"st_ps{i}", [P, TOK], F32)) for i in range(3)]
        mx_ps = [ctx.enter_context(nc.psum_tensor(f"mx_ps{i}", [P, 512], F32)) for i in range(3)]
        o_ps = ctx.enter_context(nc.psum_tensor("o_ps", [P, TOK], F32))
        sum_ps = ctx.enter_context(nc.psum_tensor("sum_ps", [P, TOK], F32))

        k_ld = [sem(f"k_ld{i}") for i in range(2)]
        q_ld = [sem(f"q_ld{i}") for i in range(QC)]
        v_ld = [sem(f"v_ld{i}") for i in range(2)]
        shift_ld, o_st = sem("shift_ld"), sem("o_st")
        zeroed, ident_ok, ones_ok = sem("zeroed_b"), sem("ident_ok_b"), sem("ones_ok")
        st_ready, unit_ready, rows_ready = sem("st_ready"), sem("unit_ready"), sem("rows_ready")
        pv_done, sum_done = sem("pv_done"), sem("sum_done")
        exp_done, o_copied, sum_copied, shift_done = sem("exp_done"), sem("o_copied"), sem("sum_copied"), sem("shift_done")
        unit_done, max_done, inv_done, o_done = sem("unit_done"), sem("max_done"), sem("inv_done"), sem("o_done")
        pair_done = sem("pair_done")

        G = 2 * QC
        TURNS = NQ // 2

        SK = 4 * KT
        STEPS = ["USUSUSVUS"] * KT
        STEPS[0] = "UVUSSUSUS"
        STEPS[AHEAD - 1] = "USUSUSUSV"
        STEPS[AHEAD] = "TSSSUSUVUU"
        FIRST = sum(s.count("U") for s in STEPS[AHEAD:])

        def unit_at(kt, i):
            steps = "".join(STEPS[AHEAD if kt >= AHEAD else 0:kt]) + STEPS[kt][:i]
            return steps.count("U") + (0 if kt >= AHEAD else FIRST)

        def units_of(kt):
            return [unit_at(kt, i) for i, step in enumerate(STEPS[kt]) if step == "U"]

        assert units_of(AHEAD - 1)[-1] == UN - 1

        with nc.Block() as block:

            @block.sync
            def _(sp):
                def load_keys(it, u):
                    for part, src in enumerate((kh_d, kh_d, kl_d)):
                        sp.dma_start(k_x[u][part * D:(part + 1) * D, :, :].bitcast(F32),
                                     src[it, :, :].rearrange("(h d) n -> d h n", d=D)).then_inc(k_ld[u], 16)

                def load_values(it, u):
                    sp.dma_start(v_sb[u][:, :, :], v_d[it, :, :, :]).then_inc(v_ld[u], 16)

                def load_queries(it, qc):
                    for part, src in enumerate((qh_d, ql_d, qh_d)):
                        sp.dma_start(q_x[qc][part * D:(part + 1) * D, :, :].bitcast(F32),
                                     src[it, :, qc * TOK:(qc + 1) * TOK].rearrange("(h d) n -> d h n", d=D)).then_inc(q_ld[qc], 16)

                def load_shift(count, qc):
                    sp.wait_ge(shift_done, count)
                    sp.dma_start(q_x[qc][R:R + 1, :, :].bitcast(F32),
                                 shift[:, :].bitcast(F32)).then_inc(shift_ld, 16)

                def store_group(turn0, it, qc, count):
                    dst = o_d[it, :, qc * TOK:(qc + 1) * TOK]
                    sp.lower_val(dst.offset * 4)
                    sp.wait_ge(o_done, count)
                    sp.dma_start(dst, o_out[:, :]).then_inc(o_st, 16)

                load_keys(0, 0)
                for qc in range(QC):
                    load_queries(0, qc)
                load_values(0, 0)
                load_shift(1, 0)

                def turn(L, first, last):
                    for g in range(G):
                        u, qc = g // QC, g % QC
                        it, more = L * 2 + u, not (last and u == 1)
                        if qc == 0 and more:
                            sp.wait_ge(pv_done, L * G * KT + g * KT)
                            load_keys(it + 1 if isinstance(it, int) else it + 1, 1 - u)
                            load_values(it + 1, 1 - u)
                        if qc > 0 and more:
                            sp.wait_ge(st_ready, L * G * SK + g * SK)
                            load_queries(it + 1, qc - 1)
                        if qc == 0 and not (first and u == 0):
                            sp.wait_ge(st_ready, L * G * SK + g * SK)
                            load_queries(it, QC - 1)
                        if not (first and g == 0):
                            store_group(L, it - 1 if qc == 0 else it, (qc - 1) % QC, L * G + g)
                        if not (last and g == G - 1):
                            load_shift(L * G + g + 2, (qc + 1) % QC)

                turn(0, True, False)
                with sp.Fori(1, TURNS - 1) as L:
                    turn(L, False, False)
                turn(TURNS - 1, False, True)
                store_group(0, NQ - 1, QC - 1, NQ * QC)
                sp.wait_ge(o_st, NQ * QC * 16)

            @block.gpsimd
            def _(pool):
                pool.memset(ident[:, :], 0.0).then_inc(zeroed, 1)
                pool.wait_ge(zeroed, 1)
                pool.affine_select(out=ident[:, :], in_=ident[:, :], compare_op=ALU.not_equal, fill=1.0, base=0,
                                   pattern=[[-1, P]], channel_multiplier=1).then_inc(ident_ok, 1)

                def turn(L):
                    for g in range(G):
                        for n, i in enumerate(ADDS):
                            done = L * G * NA + g * NA + n
                            if i == "four":
                                pool.wait_ge(pair_done, done)
                                pool.tensor_tensor(p_pair[:, 1, :, :], p_pair[:, 0, :, :], p_pair[:, 1, :, :], ALU.add).then_inc(pair_done, 1)
                                continue
                            pool.wait_ge(exp_done, L * G * SK + g * SK + 8 * i + 8)
                            if i in (2, 6):
                                pool.wait_ge(pair_done, done)
                            else:
                                pool.wait_ge(sum_done, since(L * G * NS, g * NS + {0: -1, 1: 0, 3: 1, 4: 2, 5: 3, 7: 4}[i]))
                            pool.tensor_tensor(p_pair[:, i % 2, :, :], p_sb[:, 2 * i % SLOTS, :, :], p_sb[:, (2 * i + 1) % SLOTS, :, :],
                                               ALU.add).then_inc(pair_done, 1)

                turn(0)
                with pool.Fori(1, TURNS) as L:
                    turn(L)

            @block.scalar
            def _(act):
                def turn_shift(count):
                    act.wait_ge(rows_ready, count)
                    if not (isinstance(count, int) and count == 1):
                        act.wait_ge(shift_ld, (count - 1) * 16)
                    act.activation(shift[:, :], mx_ps[1][0:4 * TT, 0:P], ACT.Copy, scale=-1.0).then_inc(shift_done, 1)

                def copy_o(count):
                    act.wait_ge(pv_done, count * KT)
                    act.wait_ge(o_done, count - 1)
                    act.activation(o_raw[:, :], o_ps[:, :], ACT.Copy).then_inc(o_copied, 1)

                def copy_sum(count):
                    act.wait_ge(sum_done, count * NS)
                    act.wait_ge(inv_done, (count - 1) * 4)
                    act.activation(sum_raw[:, :], sum_ps[:, :], ACT.Copy).then_inc(sum_copied, 1)

                turn_shift(1)

                def turn(L, first, last):
                    for g in range(G):
                        for kt in range(KT):
                            n = g * KT + kt
                            if kt == AHEAD and not (last and g == G - 1):
                                turn_shift(L * G + g + 2)
                            for h in range(4):
                                act.wait_ge(st_ready, L * G * SK + 4 * n + h + 1)
                                if h == 0:
                                    act.wait_ge(pv_done, since(L * G * KT, n - SLOTS + 1))
                                    old = n - SLOTS
                                    act.wait_ge(pair_done, since(L * G * NA, old // KT * NA + ADDS.index(old % KT // 2) + 1))
                                act.activation(p_sb[:, kt % SLOTS, h, :], st_ps[(4 * kt + h) % 3][:, :], ACT.Exp,
                                               scale=SCALE).then_inc(exp_done, 1)
                            if kt == 0 and not (first and g == 0):
                                copy_o(L * G + g)
                            if kt == 3 and not (first and g == 0):
                                copy_sum(L * G + g)

                turn(0, True, False)
                with act.Fori(1, TURNS - 1) as L:
                    turn(L, False, False)
                turn(TURNS - 1, False, True)
                copy_o(NQ * QC)
                copy_sum(NQ * QC)

            @block.vector
            def _(dve):
                def unit(base, n):
                    dve.wait_ge(unit_ready, base + n + 1)
                    dve.reduce_max(unit_max[:, n // 4, n % 4:n % 4 + 1], mx_ps[n % 3][:, :], AX.X).then_inc(unit_done, 1)

                def rows(base, count):
                    dve.wait_ge(unit_done, base + UN)
                    dve.wait_ge(rows_ready, count - 1)
                    dve.reduce_max(row_max[:, :], unit_max[:, :, :], AX.X).then_inc(max_done, 1)

                def invert(count, part):
                    cols = slice(part * P, (part + 1) * P)
                    if part == 0:
                        dve.wait_ge(sum_copied, count)
                        dve.wait_ge(o_done, count - 1)
                    dve.reciprocal(o_inv[:, cols], sum_raw[:, cols]).then_inc(inv_done, 1)

                def normalise(count):
                    dve.wait_ge(inv_done, count * 4)
                    dve.wait_ge(o_copied, count)
                    dve.wait_ge(o_st, (count - 1) * 16)
                    dve.tensor_tensor(o_out[:, :], o_raw[:, :], o_inv[:, :], ALU.mult).then_inc(o_done, 1)

                for i in range(2):
                    dve.memset(k_x[i][R:R + 1, :, :].bitcast(F32), 1.0).then_inc(ones_ok, 1)
                dve.memset(ones[:, :], 1.0).then_inc(ones_ok, 1)
                for n in range(UN):
                    unit(0, n)
                rows(0, 1)
                for n in range(FIRST):
                    if n == 0:
                        dve.wait_ge(max_done, 1)
                    unit(UN, n)

                def turn(L, first, last):
                    for g in range(G):
                        for kt in range(KT):
                            ahead = 2 if kt >= AHEAD else 1
                            if not (last and g + ahead >= G):
                                base = (L * G + g + ahead) * UN
                                for n in units_of(kt):
                                    if n == 0:
                                        dve.wait_ge(max_done, L * G + g + 2)
                                    unit(base, n)
                                if kt == AHEAD - 1:
                                    rows(base, L * G + g + 2)
                            if 4 <= kt < 8 and not (first and g == 0):
                                invert(L * G + g, kt - 4)
                            if kt == 8 and not (first and g == 0):
                                normalise(L * G + g)

                turn(0, True, False)
                with dve.Fori(1, TURNS - 1) as L:
                    turn(L, False, False)
                turn(TURNS - 1, False, True)
                for part in range(4):
                    invert(NQ * QC, part)
                normalise(NQ * QC)

            @block.tensor
            def _(pe):
                def unit(base, n, u, qc):
                    h, t, kc = n // (4 * TT), n // 4 % TT, n % 4
                    if n >= 3:
                        pe.wait_ge(unit_done, base + n - 2)
                    pe.matmul(mx_ps[n % 3][:, :], q_x[qc][0:R, h, t * P:(t + 1) * P], k_x[u][0:R, h, kc * 512:(kc + 1) * 512],
                              start=True, stop=True).then_inc(unit_ready, 1)

                def turn_rows(count):
                    pe.wait_ge(max_done, count)
                    pe.transpose(mx_ps[1][0:4 * TT, 0:P], row_max[:, :], ident[:, :]).then_inc(rows_ready, 1)

                def values(L, n, u, kt):
                    pe.wait_ge(exp_done, L * G * SK + 4 * n + 4)
                    for h in range(4):
                        rows = slice(h * D, (h + 1) * D)
                        op = pe.matmul(o_ps[rows, :], v_sb[u][:, kt, rows], p_sb[:, kt % SLOTS, h, :], start=(kt == 0), stop=(kt == KT - 1))
                    op.then_inc(pv_done, 1)

                def sums(L, g, i):
                    adds, slot, _ = PARTS[i]
                    pe.wait_ge(pair_done, L * G * NA + g * NA + adds)
                    for h in range(4):
                        op = pe.matmul(sum_ps[h * D:(h + 1) * D, :], ones[:, :], p_pair[:, slot, h, :], start=(i == 0), stop=(i == NS - 1))
                    op.then_inc(sum_done, 1)

                pe.wait_ge(ident_ok, 1)
                pe.wait_ge(ones_ok, 3)
                pe.wait_ge(k_ld[0], 48)
                pe.wait_ge(q_ld[0], 48)
                for n in range(UN):
                    unit(0, n, 0, 0)
                turn_rows(1)
                pe.wait_ge(q_ld[1], 48)
                pe.wait_ge(shift_done, 1)
                for n in range(FIRST):
                    unit(UN, n, 0, 1)

                def turn(L, first, last):
                    for g in range(G):
                        u, qc = g // QC, g % QC

                        def next_unit(kt, n):
                            ahead = 2 if kt >= AHEAD else 1
                            nu, nq = (g + ahead) % G // QC, (g + ahead) % QC
                            if last and g + ahead >= G:
                                return
                            if n == 0:
                                pe.wait_ge(q_ld[nq], (L * 2 + (g + ahead) // QC + 1) * 48)
                                pe.wait_ge(k_ld[nu], (L + 1 + (g + ahead) // G) * 48)
                            elif n == 1:
                                pe.wait_ge(shift_done, L * G + g + 2)
                            unit((L * G + g + ahead) * UN, n, nu, nq)

                        def scores(kt, h):
                            if kt == 0 and h == 0:
                                pe.wait_ge(shift_ld, (L * G + g + 1) * 16)
                            pe.wait_ge(exp_done, since(L * G * SK, g * SK + (4 * kt + h - 2 if 4 * kt + h > 2 else 0)))
                            pe.matmul(st_ps[(4 * kt + h) % 3][:, :], k_x[u][:, h, kt * P:(kt + 1) * P], q_x[qc][:, h, :],
                                      start=True, stop=True).then_inc(st_ready, 1)

                        def products(kt):
                            if kt == 0:
                                if not (first and g == 0):
                                    values(L, g * KT - 1, (g - 1) % G // QC, KT - 1)
                                return
                            if kt == 1:
                                pe.wait_ge(v_ld[u], (L + 1) * 16)
                                if not (first and g == 0):
                                    pe.wait_ge(o_copied, L * G + g)
                            values(L, g * KT + kt - 1, u, kt - 1)

                        for kt in range(KT):
                            for i, step in enumerate(STEPS[kt]):
                                if step == "U":
                                    next_unit(kt, unit_at(kt, i))
                                elif step == "S":
                                    scores(kt, STEPS[kt][:i].count("S"))
                                elif step == "V":
                                    products(kt)
                                elif not (last and g == G - 1):
                                    turn_rows(L * G + g + 2)
                            for i, (_, _, at) in enumerate(PARTS):
                                if at == kt:
                                    if i == 0 and not (first and g == 0):
                                        pe.wait_ge(sum_copied, L * G + g)
                                    sums(L, g, i)
                                elif at == kt + KT and not (first and g == 0):
                                    sums(L, g - 1, i)

                turn(0, True, False)
                with pe.Fori(1, TURNS - 1) as L:
                    turn(L, False, False)
                turn(TURNS - 1, False, True)
                values(TURNS - 1, G * KT - 1, 1, KT - 1)
                for i in range(NS):
                    if PARTS[i][2] >= KT:
                        sums(TURNS - 1, G - 1, i)


def output_stage(nc, proj_wT, o_d, y_d, out):
    NC2 = B * NCH
    ctx = ExitStack()
    with ctx:
        def sb(name, shape, dt):
            return ctx.enter_context(nc.sbuf_tensor(name, shape, dt))

        def sem(name):
            return ctx.enter_context(nc.semaphore(name))

        w_f = sb("w_f", [P, CC, C], F32)
        w_hi = sb("w_hi", [P, CC, C], F32R)
        w_lo = sb("w_lo", [P, CC, C], F32R)
        o_in = sb("o_in", [P, 4, CC, TOK], F32)
        o_hi = sb("o_hi", [P, 2, CC, TOK], F32R)
        o_lo = sb("o_lo", [P, 2, CC, TOK], F32R)
        y_in = sb("y_in", [P, 4, TT, C], F32)
        ps = [ctx.enter_context(nc.psum_tensor(f"ps{i}", [P, 512], F32)) for i in range(8)]
        w_ld, w_hi_done, w_lo_done = sem("w_ld"), sem("w_hi_done_c"), sem("w_lo_done_c")
        o_ld = [sem(f"o_ld{i}") for i in range(4)]
        y_ld = [sem(f"y_ld{i}") for i in range(4)]
        out_st = [sem(f"out_st{i}") for i in range(4)]
        hi_done, lo_done, prod_done, sum_done = sem("hi_done"), sem("lo_done"), sem("prod_done"), sem("out_added")

        with nc.Block() as block:

            @block.sync
            def _(sp):
                sp.dma_start(w_f[:, :, :], proj_wT.rearrange("(c p) n -> p c n", p=P)).then_inc(w_ld, 16)

                def load(b, i, s):
                    sp.dma_start(o_in[:, s, :, :], o_d[bass.ds(b * HQ, HQ), :, i * TOK:(i + 1) * TOK].rearrange("q p n -> p q n")).then_inc(o_ld[s], 16)
                    sp.dma_start(y_in[:, s, :, :], y_d[bass.ds(b * N + i * TOK, TOK), :].rearrange("(t p) n -> p t n", p=P)).then_inc(y_ld[s], 16)

                for i in range(3):
                    load(0, i, i)

                def turn(b, first, last):
                    for i in range(NCH):
                        n = i + 3
                        if not (last and n >= NCH):
                            if not (first and n < 4):
                                sp.wait_ge(out_st[n % 4], b * 16 + n // 4 * 16)
                            load(b + n // 4, n % 4, n % 4)
                        sp.wait_ge(sum_done, b * NCH * TT + (i + 1) * TT)
                        sp.dma_start(out[bass.ds(b * N + i * TOK, TOK), :].rearrange("(t p) n -> p t n", p=P), y_in[:, i, :, :]).then_inc(out_st[i], 16)

                turn(0, True, False)
                with sp.Fori(1, B - 1) as b:
                    turn(b, False, False)
                turn(B - 1, False, True)
                for s in range(4):
                    sp.wait_ge(out_st[s], B * 16)

            @block.scalar
            def _(act):
                act.wait_ge(w_ld, 16)
                act.activation(w_hi[:, :, :], w_f[:, :, :], ACT.Copy).then_inc(w_hi_done, 1)

                def turn(b):
                    for i in range(NCH):
                        act.wait_ge(o_ld[i], b * 16 + 16)
                        act.wait_ge(prod_done, since(b * NCH * TT, (i - 1) * TT))
                        for c in range(CC):
                            act.activation(o_hi[:, i % 2, c, :], o_in[:, i, c, :], ACT.Copy).then_inc(hi_done, 1)

                turn(0)
                with act.Fori(1, B) as b:
                    turn(b)

            @block.vector
            def _(dve):
                dve.wait_ge(w_hi_done, 1)
                dve.tensor_tensor(w_lo[:, :, :], w_f[:, :, :], w_hi[:, :, :].bitcast(F32), ALU.subtract).then_inc(w_lo_done, 1)

                def split(b, i):
                    dve.wait_ge(prod_done, since(b * NCH * TT, (i - 1) * TT))
                    for c in range(CC):
                        dve.wait_ge(hi_done, b * NCH * CC + i * CC + c + 1)
                        dve.tensor_tensor(o_lo[:, i % 2, c, :], o_in[:, i % 4, c, :], o_hi[:, i % 2, c, :].bitcast(F32),
                                          ALU.subtract).then_inc(lo_done, 1)

                split(0, 0)

                def turn(b, last):
                    for i in range(NCH):
                        if not (last and i == NCH - 1):
                            split(b, i + 1)
                        dve.wait_ge(y_ld[i], b * 16 + 16)
                        for t in range(TT):
                            n = i * TT + t
                            dve.wait_ge(prod_done, b * NCH * TT + n + 1)
                            dve.tensor_tensor(y_in[:, i, t, :], ps[n % 8][:, :], y_in[:, i, t, :], ALU.add).then_inc(sum_done, 1)

                turn(0, False)
                with dve.Fori(1, B - 1) as b:
                    turn(b, False)
                turn(B - 1, True)

            @block.tensor
            def _(pe):
                pe.wait_ge(w_lo_done, 1)

                def turn(b):
                    for i in range(NCH):
                        pe.wait_ge(lo_done, b * NCH * CC + (i + 1) * CC)
                        for t in range(TT):
                            n = i * TT + t
                            pe.wait_ge(sum_done, since(b * NCH * TT, n - 7))
                            rows = slice(t * P, (t + 1) * P)
                            for c in range(CC):
                                pe.matmul(ps[n % 8][:, :], o_hi[:, i % 2, c, rows], w_hi[:, c, :], start=(c == 0), stop=False)
                                pe.matmul(ps[n % 8][:, :], o_hi[:, i % 2, c, rows], w_lo[:, c, :], start=False, stop=False)
                                op = pe.matmul(ps[n % 8][:, :], o_lo[:, i % 2, c, rows], w_hi[:, c, :], start=False, stop=(c == CC - 1))
                            op.then_inc(prod_done, 1)

                turn(0)
                with pe.Fori(1, B) as b:
                    turn(b)


def block_kernel(nc, x, qkv_wT, qk_bT, v_b, proj_wT, proj_b, wr, br, w1, b1T, w2, b2, out):
    def scratch(name, shape):
        return nc.dram_tensor(name, shape, F32, kind="Internal").ap()

    qh_d, ql_d, kh_d, kl_d, o_d = (scratch(n, (NQ, P, N)) for n in ("q_hi_d", "q_lo_d", "k_hi_d", "k_lo_d", "o_d"))
    v_d = scratch("v_d", (NQ, P, KT, P))
    y_d = scratch("y_d", (B * N, C))
    x0 = x[:, 0, :]
    xf = x.rearrange("b n c -> (b n) c")
    of = out.rearrange("b n c -> (b n) c")
    dense_stage(nc, xf, x0, qkv_wT, qk_bT, v_b, wr, br, w1, b1T, w2, b2, proj_b, qh_d, ql_d, kh_d, kl_d, v_d, y_d)
    attention_stage(nc, qh_d, ql_d, kh_d, kl_d, v_d, o_d)
    output_stage(nc, proj_wT, o_d, y_d, of)


def kernel(**inputs):
    import numpy as np
    import concourse.bacc as bacc
    from concourse.bass_utils import run_bass_kernel_spmd

    a = {k: np.asarray(v) for k, v in inputs.items()}
    arrays = {
        "x": a["L0_attn_x"],
        "qkv_wT": a["L0_attn_qkv_w"].T,
        "qk_bT": a["L0_attn_qkv_b"][0:2 * C].reshape(2 * CC, P).T,
        "v_b": a["L0_attn_qkv_b"][2 * C:],
        "proj_wT": a["L0_attn_proj_w"].T,
        "proj_b": a["L0_attn_proj_b"],
        "wr": a["L0_ffn_Wr"],
        "br": a["L0_ffn_br"],
        "w1": a["L0_ffn_W1"],
        "b1T": a["L0_ffn_b1"].reshape(E, CC, P).transpose(0, 2, 1),
        "w2": a["L0_ffn_W2"],
        "b2": a["L0_ffn_b2"],
    }
    arrays = {k: np.ascontiguousarray(v) for k, v in arrays.items()}
    nc = bacc.Bacc("TRN2", target_bir_lowering=False, num_devices=1)
    args = [nc.dram_tensor(k, v.shape, mybir.dt.from_np(v.dtype), kind="ExternalInput").ap() for k, v in arrays.items()]
    args.append(nc.dram_tensor("out", (B, N, C), F32, kind="ExternalOutput").ap())
    block_kernel(nc, *args)
    r = run_bass_kernel_spmd(nc, [arrays], core_ids=[0])
    return r.results[0]["out"]
```

```python
import concourse.bass as bass
from concourse import mybir
from contextlib import ExitStack

F32 = mybir.dt.float32
F32R = mybir.dt.float32r
U32 = mybir.dt.uint32
ALU = mybir.AluOpType
ACT = mybir.ActivationFunctionType
AX = mybir.AxisListType

P = 128
B, N, C = 4, 2048, 512
H, D = 16, 32
E = 8
EPS = 1e-5
SCALE = float(D) ** -0.5
CC = C // P
TOK = 512
NCH = N // TOK
TT = TOK // P
HQ = H // 4
NQ = B * HQ
KT = N // P


def since(base, count):
    return max(base + count, 0) if isinstance(base, int) else base + count


def dense_stage(nc, x, x0, wqkvT, qk_bT, v_b, wr, br, w1, b1T, w2, b2, proj_b, qh_d, ql_d, kh_d, kl_d, v_d, y_d):
    NW = 3 * C
    WP = 2 * C
    ORDER = ["qk"] * 8 + ["v"] * 4 + ["h", "h", "t"] * 4
    PER = {k: ORDER.count(k) for k in ("qk", "v", "h", "t")}
    ctx = ExitStack()
    with ctx:
        def sb(name, shape, dt):
            return ctx.enter_context(nc.sbuf_tensor(name, shape, dt))

        def sem(name):
            return ctx.enter_context(nc.semaphore(name))

        wq_hi = sb("wq_hi", [P, CC, NW], F32R)
        wq_lo = sb("wq_lo", [P, CC, NW], F32R)
        we_hi = sb("we_hi", [P, 2, 2, CC, C], F32R)
        we_lo = sb("we_lo", [P, 2, 2, CC, C], F32R)
        stage = sb("stage", [P, 2, WP], F32)
        xt = sb("xt", [P, TT, C], F32)
        xnT_hi = sb("xnT_hi", [P, 2, CC, TOK], F32R)
        xnT_lo = sb("xnT_lo", [P, 2, CC, TOK], F32R)
        h_f = sb("h_f", [P, 2, TOK], F32)
        h_hi = sb("h_hi", [P, 2, TOK], F32R)
        h_lo = sb("h_lo", [P, 2, TOK], F32R)
        qk_hi = sb("qk_hi", [P, 2, TOK], F32R)
        qk_lo = sb("qk_lo", [P, 2, TOK], F32R)
        v_out = sb("v_out", [P, 2, C], F32)
        y_out = sb("y_out", [P, 2, C], F32)
        x_res = sb("x_res", [P, 2, C], F32)
        v_bias = sb("v_bias", [P, C], F32)
        p_bias = sb("p_bias", [P, C], F32)
        y_bias = sb("y_bias", [P, C], F32)
        qk_bias = sb("qk_bias", [P, 8], F32)
        b1_sb = sb("b1_sb", [P, 2, CC], F32)
        ident = sb("ident", [P, P], F32)
        stats = sb("stats", [P, TT, 6], F32)
        mean = sb("mean", [P, TT], F32)
        mean_gap = sb("mean_gap", [P, TT], F32)
        var_sum = sb("var_sum", [P, TT], F32)
        var_eps = sb("var_eps", [P, TT], F32)
        rstd = sb("rstd", [P, TT], F32)
        minus_half = sb("minus_half", [P, TT], F32)
        x0_sb = y_out[0:B, 0, :]
        x0T = sb("x0T", [P, CC, B], F32)
        wr_sb = sb("wr_sb", [P, CC, E], F32)
        br_sb = sb("br_sb", [B, E], F32)
        score = sb("score", [B, E], F32)
        top = sb("top", [B, E], F32)
        top_i = sb("top_i", [B, E], U32)
        top_row = sb("top_row", [1, B * E], U32)
        rot = [ctx.enter_context(nc.psum_tensor(f"rot{i}", [P, 512], F32)) for i in range(4)]
        acc = [ctx.enter_context(nc.psum_tensor(f"acc{i}", [P, 512], F32)) for i in range(TT)]

        const_ld, x0_ld, row_ld, zeroed, ident_ok = (sem(n) for n in ("const_ld", "x0_ld", "row_ld", "zeroed", "ident_ok"))
        x0_norm, x0_tr, x0_sbd, x0_sc, x0_step, x0_top = (
            sem(n) for n in ("x0_norm", "x0_tr", "x0_sbd", "x0_sc", "x0_step", "x0_top"))
        stage_ld = [sem(f"stage_ld{i}") for i in range(2)]
        flat_ld = [sem(f"flat_ld{i}") for i in range(3)]
        w_hi_done, w_lo_done = sem("w_hi_done"), sem("w_lo_done")
        x_ld = [sem(f"x_ld{i}") for i in range(TT)]
        ln_step, var_summed, var_ready, rstd_done, ln_done = sem("ln_step"), sem("var_summed"), sem("var_ready"), sem("rstd_done"), sem("ln_done")
        ready = {k: sem(f"{k}_ready") for k in ("qk", "v", "h", "t")}
        t_hi, t_lo = sem("t_hi"), sem("t_lo")
        qk_hi_done, qk_lo_done = sem("qk_hi_done"), sem("qk_lo_done")
        v_done, gelu_done, h_hi_done, h_lo_done, h_used = (
            sem(n) for n in ("v_done", "gelu_done", "h_hi_done", "h_lo_done", "h_used"))
        emptied = {"qk": qk_lo_done, "v": v_done, "h": gelu_done, "t": t_lo}
        o_ready, y_added, y_done = sem("o_ready"), sem("y_added"), sem("y_done")
        qk_st = [sem(f"qk_st{i}") for i in range(2)]
        v_st = [sem(f"v_st{i}") for i in range(2)]
        y_st = [sem(f"y_st{i}") for i in range(2)]
        res_ld = [sem(f"res_ld{i}") for i in range(2)]
        b1_ld, bias_half, bias_done = sem("b1_ld"), sem("bias_half"), sem("bias_done")

        NPRE = CC * NW // WP
        NEXP = 2 * 2 * CC * C // WP
        flat = [t[:, :, :].rearrange("p s n -> p (s n)") for t in (h_f, v_out, x_res)]
        pre_place = [stage[:, 0, :], stage[:, 1, :]] + flat + [stage[:, 1, :]]
        pre_ld = [stage_ld[0], stage_ld[1]] + flat_ld + [stage_ld[1]]
        wq_flat = [w[:, :, :].rearrange("p c n -> p (c n)") for w in (wq_hi, wq_lo)]
        we_flat = [w[:, :, :, :, :].rearrange("p e m c n -> p (e m c n)") for w in (we_hi, we_lo)]

        def used_bank(b, i, u, last):
            at = i * len(ORDER) + u - 4
            if last and at >= (NCH - 1) * len(ORDER) and ORDER[at % len(ORDER)] == "t":
                at -= 4
            kind = ORDER[at % len(ORDER)]
            count = (at // len(ORDER)) * PER[kind] + ORDER[: at % len(ORDER) + 1].count(kind)
            if kind == "t":
                return emptied[kind], since(b * NCH * PER[kind], count + TT)
            return emptied[kind], since(b * NCH * PER[kind], count)

        def used_hidden(b, i, j):
            if j == 1:
                return o_ready, b * NCH * TT + i * TT
            return h_used, since(b * NCH * 7, i * 7 + max(j - 1, 0))

        def bank_of_t(n):
            return n if n < TT else (8 + 4 + 3 * (n % TT) + 2) % 4

        def bank_of_h(j):
            return (8 + 4 + 3 * (j // 2) + j % 2) % 4

        with nc.Block() as block:

            @block.sync
            def _(sp):
                sp.dma_start(x0_sb, x0).then_inc(x0_ld, 16)
                for t in range(TT):
                    sp.dma_start(xt[:, t, :], x[t * P:(t + 1) * P, :]).then_inc(x_ld[t], 16)
                sp.dma_start(wr_sb[:, :, :], wr.rearrange("(c p) e -> p c e", p=P)).then_inc(const_ld, 16)
                sp.dma_start(br_sb[:, :], br.partition_broadcast(B)).then_inc(const_ld, 16)
                sp.dma_start(qk_bias[:, :], qk_bT).then_inc(const_ld, 16)
                for k in range(NPRE):
                    if k == NPRE - 1:
                        sp.wait_ge(w_lo_done, 2)
                    c, part = divmod(k * WP, NW)
                    left = min(WP, NW - part)
                    sp.dma_start(pre_place[k][:, 0:left], wqkvT[c * P:(c + 1) * P, part:part + left]).then_inc(pre_ld[k], 16)
                    if left < WP:
                        sp.dma_start(pre_place[k][:, left:WP], wqkvT[(c + 1) * P:(c + 2) * P, 0:WP - left]).then_inc(pre_ld[k], 16)
                    if k == 1:
                        sp.dma_start(v_bias[:, :], v_b.partition_broadcast(P)).then_inc(const_ld, 16)
                        sp.dma_start(p_bias[:, :], proj_b.partition_broadcast(P)).then_inc(const_ld, 16)
                sp.wait_ge(x0_top, 2)
                sp.dma_start(top_row[0:1, :].rearrange("p (b e) -> p b e", e=E), top_i[:, :]).then_inc(row_ld, 16)
                for t in range(TT):
                    sp.wait_ge(ready["t"], t + 1)
                    sp.dma_start(xt[:, t, :], x[TOK + t * P:TOK + (t + 1) * P, :]).then_inc(x_ld[t], 16)
                sp.wait_ge(row_ld, 16)

                def picked(b):
                    return [sp.value_load(top_row[0:1, bass.ds(b * E + e, 1)], min_val=0, max_val=E - 1) for e in range(2)]

                def load_piece(b, pick, m):
                    e, mat, c2 = m // 4, m // 2 % 2, m % 2
                    sp.wait_ge(w_lo_done, b * NEXP + NPRE + m - 1)
                    src = (w1, w2)[mat][bass.ds(pick[e], 1), c2 * 2 * P:(c2 + 1) * 2 * P, :]
                    sp.dma_start(stage[:, m % 2, :].rearrange("p (c n) -> p c n", n=C),
                                 src.rearrange("a (c p) n -> (a p) c n", p=P)).then_inc(stage_ld[m % 2], 16)

                for m in range(2):
                    load_piece(0, picked(0), m)

                def turn(b, last):
                    pick = picked(b)
                    sp.wait_ge(gelu_done, b * NCH * PER["h"])
                    for e in range(2):
                        sp.dma_start(b1_sb[:, e, :], b1T[bass.ds(pick[e], 1), :, :].rearrange("a p c -> (a p) c")).then_inc(b1_ld, 16)
                    sp.wait_ge(y_added, b * NCH * TT)
                    for e in range(2):
                        sp.dma_start(x_res[:, e, :], b2[bass.ds(pick[e], 1), :].rearrange("a n -> (a n)").partition_broadcast(P)).then_inc(res_ld[e], 16)
                    for i in range(NCH):
                        tok = b * N + i * TOK
                        for m in range(8):
                            hi_d, lo_d = ((qh_d, ql_d), (kh_d, kl_d))[m // 4]
                            dst = slice(i * TOK, (i + 1) * TOK)
                            sp.wait_ge(qk_lo_done, b * NCH * 8 + i * 8 + m + 1)
                            sp.dma_start(hi_d[bass.ds(b * HQ + m % 4, 1), :, dst].rearrange("a p n -> (a p) n"),
                                         qk_hi[:, m % 2, :].bitcast(F32)).then_inc(qk_st[m % 2], 16)
                            sp.dma_start(lo_d[bass.ds(b * HQ + m % 4, 1), :, dst].rearrange("a p n -> (a p) n"),
                                         qk_lo[:, m % 2, :].bitcast(F32)).then_inc(qk_st[m % 2], 16)
                            if i == 0 and m < NEXP - 2:
                                load_piece(b, pick, m + 2)
                        for t in range(TT):
                            sp.wait_ge(v_done, b * NCH * TT + i * TT + t + 1)
                            sp.dma_start(v_d[bass.ds(b * HQ, HQ), :, i * TT + t, :].rearrange("q p d -> p q d"),
                                         v_out[:, t % 2, :].rearrange("p (q d) -> p q d", d=P)).then_inc(v_st[t % 2], 16)
                        if i == NCH - 1 and not last:
                            next_pick = picked(b + 1)
                            load_piece(b + 1, next_pick, 0)
                            load_piece(b + 1, next_pick, 1)
                        if not (last and i >= NCH - 2):
                            for t in range(TT):
                                sp.wait_ge(ready["t"], b * NCH * TT + i * TT + TT + t + 1)
                                sp.dma_start(xt[:, t, :], x[bass.ds(tok + 2 * TOK + t * P, P), :]).then_inc(x_ld[t], 16)
                        for t in range(TT):
                            if i == 0 and t < 2:
                                sp.wait_ge(bias_half, b + 1)
                            else:
                                sp.wait_ge(y_added, b * NCH * TT + i * TT + t - 1)
                            sp.dma_start(x_res[:, t % 2, :], x[bass.ds(tok + t * P, P), :]).then_inc(res_ld[t % 2], 16)
                            if t >= 2:
                                sp.wait_ge(y_done, b * NCH * TT + i * TT + t - 1)
                                sp.dma_start(y_d[bass.ds(tok + (t - 2) * P, P), :], y_out[:, t % 2, :]).then_inc(y_st[t % 2], 16)
                        for t in range(TT - 2, TT):
                            sp.wait_ge(y_done, b * NCH * TT + i * TT + t + 1)
                            sp.dma_start(y_d[bass.ds(tok + t * P, P), :], y_out[:, t % 2, :]).then_inc(y_st[t % 2], 16)

                turn(0, False)
                with sp.Fori(1, B - 1) as b:
                    turn(b, False)
                turn(B - 1, True)
                for i in range(2):
                    sp.wait_ge(qk_st[i], B * NCH * 4 * 32)
                    sp.wait_ge(v_st[i], B * NCH * TT // 2 * 16)
                    sp.wait_ge(y_st[i], B * NCH * TT // 2 * 16)

            @block.gpsimd
            def _(pool):
                pool.memset(ident[:, :], 0.0).then_inc(zeroed, 1)
                pool.wait_ge(zeroed, 1)
                pool.affine_select(out=ident[:, :], in_=ident[:, :], compare_op=ALU.not_equal, fill=1.0, base=0,
                                   pattern=[[-1, P]], channel_multiplier=1).then_inc(ident_ok, 1)

                def inverse_deviation(rows, cols, count):
                    pool.wait_ge(var_ready, count)
                    pool.tensor_tensor(rstd[0:rows, 0:cols], var_eps[0:rows, 0:cols], minus_half[0:rows, 0:cols],
                                       ALU.pow).then_inc(rstd_done, 1)

                pool.memset(minus_half[:, :], -0.5).then_inc(zeroed, 1)
                pool.wait_ge(zeroed, 2)
                inverse_deviation(B, 1, 1)
                inverse_deviation(P, TT, 2)

                def turn(b, last):
                    for i in range(NCH):
                        if not (last and i == NCH - 1):
                            inverse_deviation(P, TT, b * NCH + i + 3)
                        for j in range(8):
                            n = i * 8 + j
                            pool.wait_ge(h_hi_done, b * NCH * 8 + n + 1)
                            pool.wait_ge(*used_hidden(b, i, j))
                            pool.tensor_tensor(h_lo[:, n % 2, :], h_f[:, n % 2, :], h_hi[:, n % 2, :].bitcast(F32),
                                               ALU.subtract).then_inc(h_lo_done, 1)
                        for t in range(TT):
                            n = i * TT + t
                            if n == 0:
                                pool.wait_ge(bias_done, b + 1)
                            pool.wait_ge(y_added, b * NCH * TT + n + 1)
                            pool.tensor_tensor(y_out[:, t % 2, :], y_out[:, t % 2, :], y_bias[:, :], ALU.add).then_inc(y_done, 1)

                turn(0, False)
                with pool.Fori(1, B - 1) as b:
                    turn(b, False)
                turn(B - 1, True)

            @block.scalar
            def _(act):
                def transposed_hi(b, n, s, t):
                    act.wait_ge(ready["t"], b * NCH * TT + n + 1)
                    act.activation(xnT_hi[:, s, :, t * P:(t + 1) * P],
                                   rot[bank_of_t(n)][:, :].rearrange("p (c n) -> p c n", n=P), ACT.Copy).then_inc(t_hi, 1)

                def dmas(k):
                    return 2 if (k * WP) % NW + WP > NW else 1

                for k in range(NPRE):
                    if k == 2:
                        for t in range(TT):
                            transposed_hi(0, t, 0, t)
                    act.wait_ge(pre_ld[k], 16 * (dmas(k) + (dmas(1) if k == NPRE - 1 else 0)))
                    act.activation(wq_flat[0][:, k * WP:(k + 1) * WP], pre_place[k], ACT.Copy).then_inc(w_hi_done, 1)

                def turn(b, last):
                    for i in range(NCH):
                        for m in range(8):
                            n = i * 8 + m
                            act.wait_ge(ready["qk"], b * NCH * 8 + n + 1)
                            if n == 0:
                                act.wait_ge(const_ld, 80)
                            act.wait_ge(qk_st[m % 2], since(b * NCH * 4 * 32, (n // 2) * 32))
                            act.activation(qk_hi[:, m % 2, :], rot[m % 4][:, :], ACT.Identity,
                                           bias=qk_bias[:, m:m + 1]).then_inc(qk_hi_done, 1)
                            if i == 0:
                                before = dmas(1) + dmas(NPRE - 1) if m % 2 else dmas(0)
                                act.wait_ge(stage_ld[m % 2], 16 * before + 16 * (NEXP // 2 * b + m // 2 + 1))
                                act.wait_ge(o_ready, b * NCH * TT)
                                act.activation(we_flat[0][:, m * WP:(m + 1) * WP], stage[:, m % 2, :], ACT.Copy,
                                               scale=0.5 if m // 2 % 2 else 1.0).then_inc(w_hi_done, 1)
                        for j in range(8):
                            n = i * 8 + j
                            if n == 0:
                                act.wait_ge(b1_ld, b * 32 + 32)
                            act.wait_ge(ready["h"], b * NCH * 8 + n + 1)
                            act.wait_ge(h_lo_done, since(b * NCH * 8, n - 1))
                            act.activation(h_f[:, j % 2, :], rot[bank_of_h(j)][:, :], ACT.Gelu,
                                           bias=b1_sb[:, j // 4, j % 4:j % 4 + 1]).then_inc(gelu_done, 1)
                            if j % 2 and not (last and i == NCH - 1):
                                transposed_hi(b, i * TT + TT + j // 2, (i + 1) % 2, j // 2)

                turn(0, False)
                with act.Fori(1, B - 1) as b:
                    turn(b, False)
                turn(B - 1, True)

            @block.vector
            def _(dve):
                dve.wait_ge(x0_ld, 16)
                def combine(rows, cols, stepped, count):
                    r, c = slice(0, rows), slice(0, cols)
                    dve.wait_ge(ln_step, stepped)
                    dve.tensor_tensor(mean[r, c], stats[r, c, 1], stats[r, c, 4], ALU.add).then_inc(ln_step, 1)
                    dve.tensor_tensor(mean_gap[r, c], stats[r, c, 1], stats[r, c, 4], ALU.subtract).then_inc(ln_step, 1)
                    dve.tensor_tensor(var_sum[r, c], stats[r, c, 2], stats[r, c, 5], ALU.add).then_inc(ln_step, 1)
                    dve.wait_ge(ln_step, stepped + 3)
                    dve.scalar_tensor_tensor(out=mean_gap[r, c], in0=mean_gap[r, c], scalar=C / 4.0, in1=mean_gap[r, c],
                                             op0=ALU.mult, op1=ALU.mult).then_inc(ln_step, 1)
                    dve.tensor_scalar(mean[r, c], mean[r, c], 0.5, None, ALU.mult).then_inc(ln_step, 1)
                    dve.wait_ge(ln_step, stepped + 5)
                    dve.tensor_tensor(var_eps[r, c], var_sum[r, c], mean_gap[r, c], ALU.add).then_inc(var_summed, 1)
                    dve.wait_ge(var_summed, count)
                    dve.tensor_scalar(var_eps[r, c], var_eps[r, c], 1.0 / C, EPS, ALU.mult, ALU.add).then_inc(var_ready, 1)

                dve.bn_stats(stats[0:B, 0, :], x0_sb).then_inc(ln_step, 1)
                combine(B, 1, 1, 1)
                dve.wait_ge(rstd_done, 1)
                dve.tensor_scalar(x0_sb, x0_sb, mean[0:B, 0:1], rstd[0:B, 0:1], ALU.subtract, ALU.mult).then_inc(x0_norm, 1)
                dve.wait_ge(x0_tr, 1)
                dve.tensor_copy(x0T[:, :, :], rot[0][:, 0:CC * B].rearrange("p (c b) -> p c b", b=B)).then_inc(x0_sbd, 1)

                def norm_stats(b, n, t):
                    dve.wait_ge(x_ld[t], b * NCH * 16 + (n + 1) * 16)
                    if t == 0:
                        dve.wait_ge(ln_done, b * NCH * TT + n * TT)
                    dve.bn_stats(stats[:, t, :], xt[:, t, :]).then_inc(ln_step, 1)

                def norm_combine(b, n):
                    combine(P, TT, b * NCH * 9 + n * 9 + 6 + TT, b * NCH + n + 2)

                def norm_apply(b, n, t):
                    if t == 0:
                        dve.wait_ge(rstd_done, b * NCH + n + 2)
                    dve.tensor_scalar(xt[:, t, :], xt[:, t, :], mean[:, t:t + 1], rstd[:, t:t + 1],
                                      ALU.subtract, ALU.mult).then_inc(ln_done, 1)

                def transposed_lo(b, n, s, t):
                    dve.wait_ge(t_hi, b * NCH * TT + n + 1)
                    dst = slice(t * P, (t + 1) * P)
                    dve.tensor_tensor(xnT_lo[:, s, :, dst], rot[bank_of_t(n)][:, :].rearrange("p (c n) -> p c n", n=P),
                                      xnT_hi[:, s, :, dst].bitcast(F32), ALU.subtract).then_inc(t_lo, 1)

                for t in range(TT):
                    norm_stats(0, 0, t)
                norm_combine(0, 0)
                for t in range(TT):
                    norm_apply(0, 0, t)
                for k in range(NPRE):
                    if k == 2:
                        for t in range(TT):
                            transposed_lo(0, t, 0, t)
                    dve.wait_ge(w_hi_done, k + 1)
                    dve.tensor_tensor(wq_flat[1][:, k * WP:(k + 1) * WP], pre_place[k],
                                      wq_flat[0][:, k * WP:(k + 1) * WP].bitcast(F32), ALU.subtract).then_inc(w_lo_done, 1)
                    if k == 2:
                        dve.wait_ge(x0_sc, 1)
                        dve.wait_ge(const_ld, 80)
                        dve.tensor_tensor(score[:, :], acc[0][0:B, 0:E], br_sb[:, :], ALU.add).then_inc(x0_step, 1)
                        dve.wait_ge(x0_step, 1)
                        dve.max(top[:, :], score[:, :]).then_inc(x0_top, 1)
                        dve.wait_ge(x0_top, 1)
                        dve.max_index(top_i[:, :], top[:, :], score[:, :]).then_inc(x0_top, 1)

                def turn(b, last):
                    for i in range(NCH):
                        for m in range(8):
                            n = i * 8 + m
                            dve.wait_ge(qk_hi_done, b * NCH * 8 + n + 1)
                            dve.wait_ge(qk_st[m % 2], since(b * NCH * 4 * 32, (n // 2) * 32))
                            dve.scalar_tensor_tensor(out=qk_lo[:, m % 2, :], in0=rot[m % 4][:, :], scalar=qk_bias[:, m:m + 1],
                                                     in1=qk_hi[:, m % 2, :].bitcast(F32), op0=ALU.add,
                                                     op1=ALU.subtract).then_inc(qk_lo_done, 1)
                            if i == 0:
                                dve.wait_ge(w_hi_done, NEXP * b + NPRE + m + 1)
                                dve.scalar_tensor_tensor(out=we_flat[1][:, m * WP:(m + 1) * WP], in0=stage[:, m % 2, :],
                                                         scalar=0.5 if m // 2 % 2 else 1.0,
                                                         in1=we_flat[0][:, m * WP:(m + 1) * WP].bitcast(F32),
                                                         op0=ALU.mult, op1=ALU.subtract).then_inc(w_lo_done, 1)
                            if not (last and i == NCH - 1):
                                if 1 <= m < 5:
                                    norm_stats(b, i + 1, m - 1)
                                elif m == 5:
                                    norm_combine(b, i + 1)
                                elif m >= 6:
                                    norm_apply(b, i + 1, 2 * (m - 6))
                                    norm_apply(b, i + 1, 2 * (m - 6) + 1)
                        for t in range(TT):
                            n = i * TT + t
                            dve.wait_ge(ready["v"], b * NCH * TT + n + 1)
                            dve.wait_ge(v_st[t % 2], since(b * NCH * TT // 2 * 16, (n // 2) * 16))
                            dve.tensor_tensor(v_out[:, t % 2, :], rot[t % 4][:, :], v_bias[:, :], ALU.add).then_inc(v_done, 1)
                        if i == 0:
                            for e in range(2):
                                dve.wait_ge(res_ld[e], b * (NCH * TT // 2 + 1) * 16 + 16)
                            dve.wait_ge(y_done, b * NCH * TT)
                            dve.tensor_tensor(y_bias[:, :], x_res[:, 0, :], x_res[:, 1, :], ALU.add).then_inc(bias_half, 1)
                            dve.wait_ge(bias_half, b + 1)
                            dve.scalar_tensor_tensor(out=y_bias[:, :], in0=y_bias[:, :], scalar=0.5, in1=p_bias[:, :],
                                                     op0=ALU.mult, op1=ALU.add).then_inc(bias_done, 1)
                        for j in range(8):
                            n = i * 8 + j
                            dve.wait_ge(gelu_done, b * NCH * 8 + n + 1)
                            dve.wait_ge(*used_hidden(b, i, j))
                            dve.tensor_copy(h_hi[:, j % 2, :], h_f[:, j % 2, :]).then_inc(h_hi_done, 1)
                            if j % 2 and not (last and i == NCH - 1):
                                transposed_lo(b, i * TT + TT + j // 2, (i + 1) % 2, j // 2)
                        for t in range(TT):
                            n = i * TT + t
                            dve.wait_ge(o_ready, b * NCH * TT + n + 1)
                            dve.wait_ge(res_ld[t % 2], b * (NCH * TT // 2 + 1) * 16 + (n // 2 + 2) * 16)
                            dve.wait_ge(y_st[t % 2], since(b * NCH * TT // 2 * 16, (n // 2) * 16))
                            dve.tensor_tensor(y_out[:, t % 2, :], acc[t][:, :], x_res[:, t % 2, :], ALU.add).then_inc(y_added, 1)

                turn(0, False)
                with dve.Fori(1, B - 1) as b:
                    turn(b, False)
                turn(B - 1, True)

            @block.tensor
            def _(pe):
                pe.wait_ge(ident_ok, 1)
                pe.wait_ge(x0_norm, 1)
                for c in range(CC):
                    last_op = pe.transpose(rot[0][:, c * B:(c + 1) * B], x0_sb[:, c * P:(c + 1) * P], ident[0:B, 0:B])
                last_op.then_inc(x0_tr, 1)
                pe.wait_ge(x0_sbd, 1)

                def transpose_tile(b, n, t):
                    pe.wait_ge(ln_done, b * NCH * TT + n + 1)
                    for c in range(CC):
                        op = pe.transpose(rot[bank_of_t(n)][:, c * P:(c + 1) * P], xt[:, t, c * P:(c + 1) * P], ident[:, :])
                    op.then_inc(ready["t"], 1)

                def split_product(out, pairs, start, stop):
                    for k, ((lh, ll), (rh, rl)) in enumerate(pairs):
                        pe.matmul(out, lh, rh, start=start and k == 0, stop=False)
                        pe.matmul(out, lh, rl, start=False, stop=False)
                        op = pe.matmul(out, ll, rh, start=False, stop=stop and k == len(pairs) - 1)
                    return op

                for t in range(TT):
                    transpose_tile(0, t, t)
                pe.wait_ge(const_ld, 80)
                for c in range(CC):
                    last_op = pe.matmul(acc[0][0:B, 0:E], x0T[:, c, :], wr_sb[:, c, :], start=(c == 0), stop=(c == CC - 1))
                last_op.then_inc(x0_sc, 1)
                pe.wait_ge(x0_step, 1)

                def turn(b, last):
                    for i in range(NCH):
                        s = i % 2
                        pe.wait_ge(t_hi, b * NCH * TT + (i + 1) * TT)
                        pe.wait_ge(t_lo, b * NCH * TT + (i + 1) * TT)
                        if i == 0:
                            pe.wait_ge(w_lo_done, b * NEXP + NPRE)
                        u = 0
                        for m in range(8):
                            if m > 0:
                                pe.wait_ge(*used_bank(b, i, u, last))
                            cols = slice(m * P, (m + 1) * P)
                            split_product(rot[u % 4][:, :], [((wq_hi[:, c, cols], wq_lo[:, c, cols]), (xnT_hi[:, s, c, :], xnT_lo[:, s, c, :]))
                                                             for c in range(CC)], True, True).then_inc(ready["qk"], 1)
                            u += 1
                        for t in range(TT):
                            pe.wait_ge(*used_bank(b, i, u, last))
                            rows = slice(t * P, (t + 1) * P)
                            split_product(rot[u % 4][:, :], [((xnT_hi[:, s, c, rows], xnT_lo[:, s, c, rows]), (wq_hi[:, c, 2 * C:], wq_lo[:, c, 2 * C:]))
                                                             for c in range(CC)], True, True).then_inc(ready["v"], 1)
                            u += 1
                        for j in range(9):
                            if j < 8:
                                if i == 0:
                                    pe.wait_ge(w_lo_done, b * NEXP + NPRE + (j // 4 + 1) * 4)
                                pe.wait_ge(*used_bank(b, i, u, last))
                                e, cols = j // 4, slice(j % 4 * P, (j % 4 + 1) * P)
                                split_product(rot[u % 4][:, :], [((we_hi[:, e, 0, c, cols], we_lo[:, e, 0, c, cols]), (xnT_hi[:, s, c, :], xnT_lo[:, s, c, :]))
                                                                 for c in range(CC)], True, True).then_inc(ready["h"], 1)
                                u += 1
                            if j % 2 and j < 8:
                                if not (last and i == NCH - 1):
                                    pe.wait_ge(*used_bank(b, i, u, last))
                                    transpose_tile(b, i * TT + TT + j // 2, j // 2)
                                u += 1
                            if j > 0:
                                k = j - 1
                                pe.wait_ge(h_hi_done, b * NCH * 8 + i * 8 + k + 1)
                                pe.wait_ge(h_lo_done, b * NCH * 8 + i * 8 + k + 1)
                                for t in range(TT):
                                    if k == 0:
                                        pe.wait_ge(y_added, since(b * NCH * TT, i * TT + t + 1 - TT))
                                    rows = slice(t * P, (t + 1) * P)
                                    op = split_product(acc[t][:, :], [((h_hi[:, k % 2, rows], h_lo[:, k % 2, rows]),
                                                                       (we_hi[:, k // 4, 1, k % 4, :], we_lo[:, k // 4, 1, k % 4, :]))],
                                                       k == 0, k == 7)
                                    if k == 7:
                                        op.then_inc(o_ready, 1)
                                if k < 7:
                                    op.then_inc(h_used, 1)

                turn(0, False)
                with pe.Fori(1, B - 1) as b:
                    turn(b, False)
                turn(B - 1, True)


def attention_stage(nc, qh_d, ql_d, kh_d, kl_d, v_d, o_d):
    R = 3 * D
    QC = N // TOK
    UN = 4 * TT * (N // 512)
    PR = KT // 2
    INV = 8
    SLOTS = 8
    AHEAD = 13
    ADDS = [(0, 0, -2), (1, 1, -3), ("four", 1, None), (2, 0, None), (3, 2, -1), ("four", 2, None),
            (4, 0, None), (5, 1, 0), ("four", 1, None), (6, 0, None), (7, 2, 1)]
    PARTS = [(3, 1, 7), (6, 2, 11), (9, 1, 16), (10, 0, 17), (11, 2, 19)]
    PAIR_ADDED = [[pair for pair, _, _ in ADDS].index(i) + 1 for i in range(PR)]
    NA, NS = len(ADDS), len(PARTS)
    ctx = ExitStack()
    with ctx:
        def sb(name, shape, dt):
            return ctx.enter_context(nc.sbuf_tensor(name, shape, dt))

        def sem(name):
            return ctx.enter_context(nc.semaphore(name))

        k_x = [sb(f"k_x{i}", [R + 1, 4, N], F32R) for i in range(2)]
        q_x = [sb(f"q_x{i}", [R + 1, 4, TOK], F32R) for i in range(QC)]
        v_sb = [sb(f"v_sb{i}", [P, KT, P], F32) for i in range(2)]
        p_sb = sb("p_sb", [P, SLOTS, 4, TOK], F32)
        p_pair = sb("p_pair", [P, 3, 4, TOK], F32)
        ones = sb("ones", [P, D], F32)
        ident = sb("ident_b", [P, P], F32)
        unit_max = sb("unit_max", [P, 4 * TT, N // 512], F32)
        row_max = sb("row_max", [P, 4 * TT], F32)
        shift = sb("shift", [4 * TT, P], F32R)
        o_raw = sb("o_raw", [P, TOK], F32)
        sum_raw = sb("sum_raw", [P, TOK], F32)
        o_inv = sb("o_inv", [P, TOK], F32)
        st_ps = [ctx.enter_context(nc.psum_tensor(f"st_ps{i}", [P, TOK], F32)) for i in range(3)]
        mx_ps = [ctx.enter_context(nc.psum_tensor(f"mx_ps{i}", [P, 512], F32)) for i in range(3)]
        o_ps = ctx.enter_context(nc.psum_tensor("o_ps", [P, TOK], F32))
        sum_ps = ctx.enter_context(nc.psum_tensor("sum_ps", [P, TOK], F32))

        k_ld = [sem(f"k_ld{i}") for i in range(2)]
        head_ld = [sem(f"head_ld{i}") for i in range(4)]
        q_ld = [sem(f"q_ld{i}") for i in range(QC)]
        v_ld = [sem(f"v_ld{i}") for i in range(2)]
        shift_ld, o_st = sem("shift_ld"), sem("o_st")
        zeroed, ident_ok, ones_ok = sem("zeroed_b"), sem("ident_ok_b"), sem("ones_ok")
        st_ready, unit_ready, rows_ready = sem("st_ready"), sem("unit_ready"), sem("rows_ready")
        pv_done, sum_done = sem("pv_done"), sem("sum_done")
        exp_done, o_copied, sum_copied, shift_done = sem("exp_done"), sem("o_copied"), sem("sum_copied"), sem("shift_done")
        unit_done, max_done, inv_done, o_done = sem("unit_done"), sem("max_done"), sem("inv_done"), sem("o_done")
        pair_done = sem("pair_done")

        G = 2 * QC
        TURNS = NQ // 2

        SK = 4 * KT
        STEPS = [
            "UZVSUSUSUS", "USUSZUSVUS", "USUSUSVUS", "USUSUSVUSUZ",
            "USUSUSVUS", "USUSUSVUS", "USUSUSVUS", "USUSUSVUSUZ",
            "USUSUSVUS", "USUSUSVUS", "USUSUSVUS", "USUSUSVUSUZ",
            "USUSUSUSV", "SSTVSUSU", "SUSUSVUS", "USUSUSVUS",
        ]
        assert all(("Z" in STEPS[kt]) == (kt in [at % KT for _, _, at in PARTS]) for kt in range(KT))
        FIRST = sum(s.count("U") for s in STEPS[AHEAD:])

        def unit_at(kt, i):
            steps = "".join(STEPS[AHEAD if kt >= AHEAD else 0:kt]) + STEPS[kt][:i]
            return steps.count("U") + (0 if kt >= AHEAD else FIRST)

        def units_of(kt):
            return [unit_at(kt, i) for i, step in enumerate(STEPS[kt]) if step == "U"]

        assert units_of(AHEAD - 1)[-1] == UN - 1

        with nc.Block() as block:

            @block.sync
            def _(sp):
                def load_keys(it, u):
                    for part, src in enumerate((kh_d, kh_d, kl_d)):
                        sp.dma_start(k_x[u][part * D:(part + 1) * D, :, :].bitcast(F32),
                                     src[it, :, :].rearrange("(h d) n -> d h n", d=D)).then_inc(k_ld[u], 16)

                def load_values(it, u):
                    sp.dma_start(v_sb[u][:, :, :], v_d[it, :, :, :]).then_inc(v_ld[u], 16)

                def load_queries(it, qc):
                    for part, src in enumerate((qh_d, ql_d, qh_d)):
                        sp.dma_start(q_x[qc][part * D:(part + 1) * D, :, :].bitcast(F32),
                                     src[it, :, qc * TOK:(qc + 1) * TOK].rearrange("(h d) n -> d h n", d=D)).then_inc(q_ld[qc], 16)

                def load_shift(count, qc):
                    sp.wait_ge(shift_done, count)
                    sp.dma_start(q_x[qc][R:R + 1, :, :].bitcast(F32),
                                 shift[:, :].bitcast(F32)).then_inc(shift_ld, 16)

                def store_group(turn0, it, qc, count):
                    dst = o_d[it, :, qc * TOK:(qc + 1) * TOK]
                    sp.lower_val(dst.offset * 4)
                    sp.wait_ge(o_done, count)
                    sp.dma_start(dst, o_inv[:, :]).then_inc(o_st, 16)

                load_queries(0, 0)
                for h in range(4):
                    for part, src in enumerate((kh_d, kh_d, kl_d)):
                        sp.dma_start(k_x[0][part * D:(part + 1) * D, h, :].bitcast(F32), src[0, h * D:(h + 1) * D, :]).then_inc(head_ld[h], 16)
                for qc in range(1, QC):
                    load_queries(0, qc)
                load_values(0, 0)
                load_shift(1, 0)

                def turn(L, first, last):
                    for g in range(G):
                        u, qc = g // QC, g % QC
                        it, more = L * 2 + u, not (last and u == 1)
                        if qc == 0 and more:
                            sp.wait_ge(pv_done, L * G * KT + g * KT)
                            load_keys(it + 1, 1 - u)
                            load_values(it + 1, 1 - u)
                        if qc > 0 and more:
                            sp.wait_ge(st_ready, L * G * SK + g * SK)
                            load_queries(it + 1, qc - 1)
                        if qc == 0 and not (first and u == 0):
                            sp.wait_ge(st_ready, L * G * SK + g * SK)
                            load_queries(it, QC - 1)
                        if not (first and g == 0):
                            store_group(L, it - 1 if qc == 0 else it, (qc - 1) % QC, L * G + g)
                        if not (last and g == G - 1):
                            load_shift(L * G + g + 2, (qc + 1) % QC)

                turn(0, True, False)
                with sp.Fori(1, TURNS - 1) as L:
                    turn(L, False, False)
                turn(TURNS - 1, False, True)
                store_group(0, NQ - 1, QC - 1, NQ * QC)
                sp.wait_ge(o_st, NQ * QC * 16)

            @block.gpsimd
            def _(pool):
                pool.memset(ident[:, :], 0.0).then_inc(zeroed, 1)
                pool.wait_ge(zeroed, 1)
                pool.affine_select(out=ident[:, :], in_=ident[:, :], compare_op=ALU.not_equal, fill=1.0, base=0,
                                   pattern=[[-1, P]], channel_multiplier=1).then_inc(ident_ok, 1)
                pool.wait_ge(ident_ok, 1)
                pool.memset(ones[:, :], 1.0).then_inc(ones_ok, 1)
                for i in range(2):
                    pool.wait_ge(ones_ok, i + 1)
                    pool.memset(k_x[i][R:R + 1, :, :].bitcast(F32), 1.0).then_inc(ones_ok, 1)
                pool.wait_ge(ones_ok, 3)

                def turn(L):
                    for g in range(G):
                        for n, (i, slot, part) in enumerate(ADDS):
                            done = L * G * NA + g * NA + n
                            if i == "four":
                                pool.wait_ge(pair_done, done)
                                pool.tensor_tensor(p_pair[:, slot, :, :], p_pair[:, 0, :, :], p_pair[:, slot, :, :],
                                                   ALU.add).then_inc(pair_done, 1)
                                continue
                            pool.wait_ge(exp_done, L * G * SK + g * SK + 8 * i + 8)
                            if part is None:
                                pool.wait_ge(pair_done, done)
                            else:
                                pool.wait_ge(sum_done, since(L * G * NS, g * NS + part + 1))
                            pool.tensor_tensor(p_pair[:, slot, :, :], p_sb[:, 2 * i % SLOTS, :, :], p_sb[:, (2 * i + 1) % SLOTS, :, :],
                                               ALU.add).then_inc(pair_done, 1)

                turn(0)
                with pool.Fori(1, TURNS) as L:
                    turn(L)

            @block.scalar
            def _(act):
                def turn_shift(count):
                    act.wait_ge(rows_ready, count)
                    if not (isinstance(count, int) and count == 1):
                        act.wait_ge(shift_ld, (count - 1) * 16)
                    act.activation(shift[:, :], mx_ps[1][0:4 * TT, 0:P], ACT.Copy, scale=-1.0).then_inc(shift_done, 1)

                def copy_o(count):
                    act.wait_ge(pv_done, count * KT)
                    act.wait_ge(o_done, count - 1)
                    act.activation(o_raw[:, :], o_ps[:, :], ACT.Copy).then_inc(o_copied, 1)

                def copy_sum(count):
                    act.wait_ge(sum_done, count * NS)
                    act.wait_ge(inv_done, (count - 1) * INV)
                    act.activation(sum_raw[:, :], sum_ps[:, :], ACT.Copy).then_inc(sum_copied, 1)

                turn_shift(1)

                def turn(L, first, last):
                    for g in range(G):
                        for kt in range(KT):
                            n = g * KT + kt
                            if kt == 0 and not (first and g == 0):
                                copy_o(L * G + g)
                            for h in range(4):
                                if kt == AHEAD and h == 2 and not (last and g == G - 1):
                                    turn_shift(L * G + g + 2)
                                act.wait_ge(st_ready, L * G * SK + 4 * n + h + 1)
                                if h == 0:
                                    act.wait_ge(pv_done, since(L * G * KT, n - SLOTS + 1))
                                    old = n - SLOTS
                                    act.wait_ge(pair_done, since(L * G * NA, old // KT * NA + PAIR_ADDED[old % KT // 2]))
                                act.activation(p_sb[:, kt % SLOTS, h, :], st_ps[(4 * kt + h) % 3][:, :], ACT.Exp,
                                               scale=SCALE).then_inc(exp_done, 1)
                            if kt == 3 and not (first and g == 0):
                                copy_sum(L * G + g)

                turn(0, True, False)
                with act.Fori(1, TURNS - 1) as L:
                    turn(L, False, False)
                turn(TURNS - 1, False, True)
                copy_o(NQ * QC)
                copy_sum(NQ * QC)

            @block.vector
            def _(dve):
                def unit(base, n):
                    dve.wait_ge(unit_ready, base + n + 1)
                    dve.reduce_max(unit_max[:, n // 4, n % 4:n % 4 + 1], mx_ps[n % 3][:, :], AX.X).then_inc(unit_done, 1)

                def rows(base, count):
                    dve.wait_ge(unit_done, base + UN)
                    dve.wait_ge(rows_ready, count - 1)
                    dve.reduce_max(row_max[:, :], unit_max[:, :, :], AX.X).then_inc(max_done, 1)

                def invert(count, part):
                    cols = slice(part * TOK // INV, (part + 1) * TOK // INV)
                    if part == 0:
                        dve.wait_ge(sum_copied, count)
                        dve.wait_ge(o_st, (count - 1) * 16)
                    dve.reciprocal(o_inv[:, cols], sum_raw[:, cols]).then_inc(inv_done, 1)

                def normalise(count):
                    dve.wait_ge(inv_done, count * INV)
                    dve.wait_ge(o_copied, count)
                    dve.tensor_tensor(o_inv[:, :], o_raw[:, :], o_inv[:, :], ALU.mult).then_inc(o_done, 1)

                for n in range(UN):
                    unit(0, n)
                rows(0, 1)
                for n in range(FIRST):
                    if n == 0:
                        dve.wait_ge(max_done, 1)
                    unit(UN, n)

                def turn(L, first, last):
                    for g in range(G):
                        for kt in range(KT):
                            ahead = 2 if kt >= AHEAD else 1
                            if not (last and g + ahead >= G):
                                base = (L * G + g + ahead) * UN
                                for n in units_of(kt):
                                    if n == 0:
                                        dve.wait_ge(max_done, L * G + g + 2)
                                    unit(base, n)
                                if kt == AHEAD - 1:
                                    rows(base, L * G + g + 2)
                            if 4 <= kt < 4 + INV and not (first and g == 0):
                                invert(L * G + g, kt - 4)
                            if kt == AHEAD and not (first and g == 0):
                                normalise(L * G + g)

                turn(0, True, False)
                with dve.Fori(1, TURNS - 1) as L:
                    turn(L, False, False)
                turn(TURNS - 1, False, True)
                for part in range(INV):
                    invert(NQ * QC, part)
                normalise(NQ * QC)

            @block.tensor
            def _(pe):
                def unit(base, n, u, qc):
                    h, t, kc = n // (4 * TT), n // 4 % TT, n % 4
                    if n >= 3:
                        pe.wait_ge(unit_done, base + n - 2)
                    pe.matmul(mx_ps[n % 3][:, :], q_x[qc][0:R, h, t * P:(t + 1) * P], k_x[u][0:R, h, kc * 512:(kc + 1) * 512],
                              start=True, stop=True).then_inc(unit_ready, 1)

                def turn_rows(count):
                    pe.wait_ge(max_done, count)
                    pe.transpose(mx_ps[1][0:4 * TT, 0:P], row_max[:, :], ident[:, :]).then_inc(rows_ready, 1)

                def values(L, n, u, kt):
                    pe.wait_ge(exp_done, L * G * SK + 4 * n + 4)
                    for h in range(4):
                        rows = slice(h * D, (h + 1) * D)
                        op = pe.matmul(o_ps[rows, :], v_sb[u][:, kt, rows], p_sb[:, kt % SLOTS, h, :], start=(kt == 0), stop=(kt == KT - 1))
                    op.then_inc(pv_done, 1)

                def sums(L, g, i):
                    adds, slot, _ = PARTS[i]
                    pe.wait_ge(pair_done, L * G * NA + g * NA + adds)
                    for h in range(4):
                        op = pe.matmul(sum_ps[h * D:(h + 1) * D, :], ones[:, :], p_pair[:, slot, h, :], start=(i == 0), stop=(i == NS - 1))
                    op.then_inc(sum_done, 1)

                pe.wait_ge(q_ld[0], 48)
                for n in range(UN):
                    if n % (4 * TT) == 0:
                        pe.wait_ge(head_ld[n // (4 * TT)], 48)
                    unit(0, n, 0, 0)
                pe.wait_ge(ident_ok, 1)
                turn_rows(1)
                pe.wait_ge(ones_ok, 3)
                pe.wait_ge(q_ld[1], 48)
                pe.wait_ge(shift_done, 1)
                for n in range(FIRST):
                    unit(UN, n, 0, 1)

                def turn(L, first, last):
                    for g in range(G):
                        u, qc = g // QC, g % QC

                        def next_unit(kt, n):
                            ahead = 2 if kt >= AHEAD else 1
                            nu, nq = (g + ahead) % G // QC, (g + ahead) % QC
                            if last and g + ahead >= G:
                                return
                            if n == 0:
                                pe.wait_ge(q_ld[nq], (L * 2 + (g + ahead) // QC + 1) * 48)
                                if (g + ahead) // QC > 0 or not first:
                                    pe.wait_ge(k_ld[nu], (L + (g + ahead) // G + nu) * 48)
                            elif n == 1:
                                pe.wait_ge(shift_done, L * G + g + 2)
                            unit((L * G + g + ahead) * UN, n, nu, nq)

                        def scores(kt, h):
                            if kt == 0 and h == 0:
                                pe.wait_ge(shift_ld, (L * G + g + 1) * 16)
                            pe.wait_ge(exp_done, since(L * G * SK, g * SK + (4 * kt + h - 2 if 4 * kt + h > 2 else 0)))
                            pe.matmul(st_ps[(4 * kt + h) % 3][:, :], k_x[u][:, h, kt * P:(kt + 1) * P], q_x[qc][:, h, :],
                                      start=True, stop=True).then_inc(st_ready, 1)

                        def products(kt):
                            if kt == 0:
                                if not (first and g == 0):
                                    values(L, g * KT - 1, (g - 1) % G // QC, KT - 1)
                                return
                            if kt == 1:
                                pe.wait_ge(v_ld[u], (L + 1) * 16)
                                if not (first and g == 0):
                                    pe.wait_ge(o_copied, L * G + g)
                            values(L, g * KT + kt - 1, u, kt - 1)

                        def sum_part(kt):
                            for i, (_, _, at) in enumerate(PARTS):
                                if at == kt:
                                    if i == 0 and not (first and g == 0):
                                        pe.wait_ge(sum_copied, L * G + g)
                                    sums(L, g, i)
                                elif at == kt + KT and not (first and g == 0):
                                    sums(L, g - 1, i)

                        for kt in range(KT):
                            for i, step in enumerate(STEPS[kt]):
                                if step == "U":
                                    next_unit(kt, unit_at(kt, i))
                                elif step == "S":
                                    scores(kt, STEPS[kt][:i].count("S"))
                                elif step == "V":
                                    products(kt)
                                elif step == "Z":
                                    sum_part(kt)
                                elif not (last and g == G - 1):
                                    turn_rows(L * G + g + 2)

                turn(0, True, False)
                with pe.Fori(1, TURNS - 1) as L:
                    turn(L, False, False)
                turn(TURNS - 1, False, True)
                values(TURNS - 1, G * KT - 1, 1, KT - 1)
                for i in range(NS):
                    if PARTS[i][2] >= KT:
                        sums(TURNS - 1, G - 1, i)


def output_stage(nc, proj_wT, o_d, y_d, out):
    NC2 = B * NCH
    ctx = ExitStack()
    with ctx:
        def sb(name, shape, dt):
            return ctx.enter_context(nc.sbuf_tensor(name, shape, dt))

        def sem(name):
            return ctx.enter_context(nc.semaphore(name))

        w_f = sb("w_f", [P, CC, C], F32)
        w_hi = sb("w_hi", [P, CC, C], F32R)
        w_lo = sb("w_lo", [P, CC, C], F32R)
        o_in = sb("o_in", [P, 4, CC, TOK], F32)
        o_hi = sb("o_hi", [P, 2, CC, TOK], F32R)
        o_lo = sb("o_lo", [P, 2, CC, TOK], F32R)
        y_in = sb("y_in", [P, 4, TT, C], F32)
        ps = [ctx.enter_context(nc.psum_tensor(f"ps{i}", [P, 512], F32)) for i in range(8)]
        w_ld = [sem(f"w_ld{c}") for c in range(CC)]
        w_hi_done, w_lo_done = sem("w_hi_done_c"), sem("w_lo_done_c")
        o_ld = [sem(f"o_ld{i}") for i in range(4)]
        y_ld = [sem(f"y_ld{i}") for i in range(4)]
        out_st = [sem(f"out_st{i}") for i in range(4)]
        hi_done, lo_done, prod_done, sum_done = sem("hi_done"), sem("lo_done"), sem("prod_done"), sem("out_added")

        with nc.Block() as block:

            @block.sync
            def _(sp):
                for c in range(CC):
                    sp.dma_start(w_f[:, c, :], proj_wT[c * P:(c + 1) * P, :]).then_inc(w_ld[c], 16)

                def load_o(b, i):
                    sp.dma_start(o_in[:, i, :, :], o_d[bass.ds(b * HQ, HQ), :, i * TOK:(i + 1) * TOK].rearrange("q p n -> p q n")).then_inc(o_ld[i], 16)

                def load_y(b, i):
                    sp.dma_start(y_in[:, i, :, :], y_d[bass.ds(b * N + i * TOK, TOK), :].rearrange("(t p) n -> p t n", p=P)).then_inc(y_ld[i], 16)

                for i in range(NCH):
                    load_o(0, i)
                    load_y(0, i)

                def turn(b, first, last):
                    for i in range(NCH):
                        if not last:
                            sp.wait_ge(lo_done, b * NCH * CC + (i + 1) * CC)
                            load_o(b + 1, i)
                        sp.wait_ge(sum_done, b * NCH * TT + (i + 1) * TT)
                        sp.dma_start(out[bass.ds(b * N + i * TOK, TOK), :].rearrange("(t p) n -> p t n", p=P), y_in[:, i, :, :]).then_inc(out_st[i], 16)
                        if i == 0 and not first:
                            sp.wait_ge(out_st[NCH - 1], b * 16)
                            load_y(b, NCH - 1)
                        elif i > 0 and not last:
                            sp.wait_ge(out_st[i - 1], b * 16 + 16)
                            load_y(b + 1, i - 1)

                turn(0, True, False)
                with sp.Fori(1, B - 1) as b:
                    turn(b, False, False)
                turn(B - 1, False, True)
                for s in range(4):
                    sp.wait_ge(out_st[s], B * 16)

            @block.scalar
            def _(act):
                for c in range(CC):
                    act.wait_ge(w_ld[c], 16)
                    act.activation(w_hi[:, c, :], w_f[:, c, :], ACT.Copy).then_inc(w_hi_done, 1)

                def turn(b):
                    for i in range(NCH):
                        act.wait_ge(o_ld[i], b * 16 + 16)
                        act.wait_ge(prod_done, since(b * NCH * TT, (i - 1) * TT))
                        for c in range(CC):
                            act.activation(o_hi[:, i % 2, c, :], o_in[:, i, c, :], ACT.Copy).then_inc(hi_done, 1)

                turn(0)
                with act.Fori(1, B) as b:
                    turn(b)

            @block.vector
            def _(dve):
                for c in range(CC):
                    dve.wait_ge(w_hi_done, c + 1)
                    dve.tensor_tensor(w_lo[:, c, :], w_f[:, c, :], w_hi[:, c, :].bitcast(F32), ALU.subtract).then_inc(w_lo_done, 1)

                def split(b, i):
                    dve.wait_ge(prod_done, since(b * NCH * TT, (i - 1) * TT))
                    for c in range(CC):
                        dve.wait_ge(hi_done, b * NCH * CC + i * CC + c + 1)
                        dve.tensor_tensor(o_lo[:, i % 2, c, :], o_in[:, i % 4, c, :], o_hi[:, i % 2, c, :].bitcast(F32),
                                          ALU.subtract).then_inc(lo_done, 1)

                split(0, 0)

                def turn(b, last):
                    for i in range(NCH):
                        if not (last and i == NCH - 1):
                            split(b, i + 1)
                        dve.wait_ge(y_ld[i], b * 16 + 16)
                        for t in range(TT):
                            n = i * TT + t
                            dve.wait_ge(prod_done, b * NCH * TT + n + 1)
                            dve.tensor_tensor(y_in[:, i, t, :], ps[n % 8][:, :], y_in[:, i, t, :], ALU.add).then_inc(sum_done, 1)

                turn(0, False)
                with dve.Fori(1, B - 1) as b:
                    turn(b, False)
                turn(B - 1, True)

            @block.tensor
            def _(pe):
                pe.wait_ge(w_lo_done, CC)

                def turn(b):
                    for i in range(NCH):
                        pe.wait_ge(lo_done, b * NCH * CC + (i + 1) * CC)
                        for t in range(TT):
                            n = i * TT + t
                            pe.wait_ge(sum_done, since(b * NCH * TT, n - 7))
                            rows = slice(t * P, (t + 1) * P)
                            for c in range(CC):
                                pe.matmul(ps[n % 8][:, :], o_hi[:, i % 2, c, rows], w_hi[:, c, :], start=(c == 0), stop=False)
                                pe.matmul(ps[n % 8][:, :], o_hi[:, i % 2, c, rows], w_lo[:, c, :], start=False, stop=False)
                                op = pe.matmul(ps[n % 8][:, :], o_lo[:, i % 2, c, rows], w_hi[:, c, :], start=False, stop=(c == CC - 1))
                            op.then_inc(prod_done, 1)

                turn(0)
                with pe.Fori(1, B) as b:
                    turn(b)


def block_kernel(nc, x, qkv_wT, qk_bT, v_b, proj_wT, proj_b, wr, br, w1, b1T, w2, b2, out):
    def scratch(name, shape):
        return nc.dram_tensor(name, shape, F32, kind="Internal").ap()

    qh_d, ql_d, kh_d, kl_d, o_d = (scratch(n, (NQ, P, N)) for n in ("q_hi_d", "q_lo_d", "k_hi_d", "k_lo_d", "o_d"))
    v_d = scratch("v_d", (NQ, P, KT, P))
    y_d = scratch("y_d", (B * N, C))
    x0 = x[:, 0, :]
    xf = x.rearrange("b n c -> (b n) c")
    of = out.rearrange("b n c -> (b n) c")
    dense_stage(nc, xf, x0, qkv_wT, qk_bT, v_b, wr, br, w1, b1T, w2, b2, proj_b, qh_d, ql_d, kh_d, kl_d, v_d, y_d)
    attention_stage(nc, qh_d, ql_d, kh_d, kl_d, v_d, o_d)
    output_stage(nc, proj_wT, o_d, y_d, of)


def kernel(**inputs):
    import numpy as np
    import concourse.bacc as bacc
    from concourse.bass_utils import run_bass_kernel_spmd

    a = {k: np.asarray(v) for k, v in inputs.items()}
    arrays = {
        "x": a["L0_attn_x"],
        "qkv_wT": a["L0_attn_qkv_w"].T,
        "qk_bT": a["L0_attn_qkv_b"][0:2 * C].reshape(2 * CC, P).T,
        "v_b": a["L0_attn_qkv_b"][2 * C:],
        "proj_wT": a["L0_attn_proj_w"].T,
        "proj_b": a["L0_attn_proj_b"],
        "wr": a["L0_ffn_Wr"],
        "br": a["L0_ffn_br"],
        "w1": a["L0_ffn_W1"],
        "b1T": a["L0_ffn_b1"].reshape(E, CC, P).transpose(0, 2, 1),
        "w2": a["L0_ffn_W2"],
        "b2": a["L0_ffn_b2"],
    }
    arrays = {k: np.ascontiguousarray(v) for k, v in arrays.items()}
    nc = bacc.Bacc("TRN2", target_bir_lowering=False, num_devices=1)
    args = [nc.dram_tensor(k, v.shape, mybir.dt.from_np(v.dtype), kind="ExternalInput").ap() for k, v in arrays.items()]
    args.append(nc.dram_tensor("out", (B, N, C), F32, kind="ExternalOutput").ap())
    block_kernel(nc, *args)
    r = run_bass_kernel_spmd(nc, [arrays], core_ids=[0])
    return r.results[0]["out"]
```
